# Optimizing a Trainium2 kernel written in Bass

```python
import numpy as np
import jax
import jax.numpy as jnp

def _softmax(x, axis=-1):
    return jax.nn.softmax(x, axis=axis)

def _gelu(x):
    return jax.nn.gelu(x, approximate=True)

def _silu(x):
    return jax.nn.silu(x)

def _sigmoid(x):
    return jax.nn.sigmoid(x)

def _layernorm(x, axis=-1, eps=1e-05):
    m = jnp.mean(x, axis=axis, keepdims=True)
    v = jnp.var(x, axis=axis, keepdims=True)
    return (x - m) / jnp.sqrt(v + eps)

def _scatter_add(tgt, idx, src, axis=0):
    return tgt.at[idx].add(src)

def _segment_sum(src, seg, n):
    return jax.ops.segment_sum(src, seg, n)
kernel_name = 'mk_gnn_preln_d4_gnn_r16_87b0ba'

def setup_inputs(seed: int=0):
    np.random.seed(seed)
    _w = jnp.asarray

    def _rec_inputs():
        import jax
        import jax.numpy as jnp
        _gk = jax.random.key(seed)
        x = 0.0001712 + 1 * jax.random.normal(jax.random.fold_in(_gk, 1), (6250, 16), jnp.float32)
        _s = jax.random.randint(jax.random.fold_in(_gk, 2), (100000,), 0, 6250, jnp.int32)
        _d = jax.random.randint(jax.random.fold_in(_gk, 3), (100000,), 0, 6250, jnp.int32)
        _loop = jnp.arange(6250, dtype=jnp.int32)
        src = jnp.concatenate([_s, _d, _loop])
        dst = jnp.concatenate([_d, _s, _loop])
        _o = jnp.argsort(dst, stable=True)
        src = src[_o]
        dst = dst[_o]
        edge_attr_16 = -0.00010739 + 0.99994 * jax.random.normal(jax.random.fold_in(_gk, 12), (206250, 16), jnp.float32)
        edge_type_8 = jax.random.randint(jax.random.fold_in(_gk, 14), (206250,), 0, 8, jnp.int32)
        edge_type_90 = jax.random.randint(jax.random.fold_in(_gk, 15), (206250,), 0, 90, jnp.int32)
        return (x, src, dst, edge_attr_16, edge_type_8, edge_type_90)
    x, src, dst, edge_attr_16, edge_type_8, edge_type_90 = _rec_inputs()

    def _L0_gnn_setup():
        import jax, jax.numpy as jnp
        import numpy as np
        N = 3125
        E = 25000
        IN_CH = 16
        SLOPE = 0.01

        def leaky(v):
            return jnp.where(v > 0, v, SLOPE * v)

        def gcn_conv(x, src, dst, W, b, n):
            h = x @ W
            deg = jnp.zeros((n,), x.dtype).at[dst].add(1.0) + 1.0
            dinv = jax.lax.rsqrt(deg)
            norm = dinv[src] * dinv[dst]
            agg = jax.ops.segment_sum(h[src] * norm[:, None], dst, num_segments=n)
            agg = agg + h * (dinv * dinv)[:, None]
            return agg + b
        key = jax.random.key(seed)
        ks = jax.random.split(key, 24)

        def w(k, i, o):
            return jax.random.normal(k, (i, o), jnp.float32) / np.sqrt(i)
        inp = {'x': jax.random.normal(ks[0], (N, IN_CH), jnp.float32), 'edge_index': jax.random.randint(ks[1], (2, E), 0, N, jnp.int64), 'enc_W0': w(ks[2], IN_CH, 64), 'enc_b0': jnp.zeros((64,), jnp.float32), 'enc_W1': w(ks[3], 64, 128), 'enc_b1': jnp.zeros((128,), jnp.float32), 'enc_W2': w(ks[4], 128, 64), 'enc_b2': jnp.zeros((64,), jnp.float32), 'lat_W0': w(ks[5], 64, 32), 'lat_b0': jnp.zeros((32,), jnp.float32), 'lat_W1': w(ks[6], 32, 3), 'lat_b1': jnp.zeros((3,), jnp.float32), 'dfc_W0': w(ks[7], 3, 32), 'dfc_b0': jnp.zeros((32,), jnp.float32), 'dfc_W1': w(ks[8], 32, 64), 'dfc_b1': jnp.zeros((64,), jnp.float32), 'dec_W0': w(ks[9], 64, 128), 'dec_b0': jnp.zeros((128,), jnp.float32), 'dec_W1': w(ks[10], 128, 64), 'dec_b1': jnp.zeros((64,), jnp.float32), 'dec_W2': w(ks[11], 64, IN_CH), 'dec_b2': jnp.zeros((IN_CH,), jnp.float32)}
        return inp
    _L0_gnn_all = _L0_gnn_setup()
    _L0_gnn_in = {k: v for k, v in _L0_gnn_all.items() if k in ('enc_W0', 'enc_b0', 'enc_W1', 'enc_b1', 'enc_W2', 'enc_b2', 'lat_W0', 'lat_b0', 'lat_W1', 'lat_b1', 'dfc_W0', 'dfc_b0', 'dfc_W1', 'dfc_b1', 'dec_W0', 'dec_b0', 'dec_W1', 'dec_b1', 'dec_W2', 'dec_b2')}
    del _L0_gnn_all

    def _L1_gnn_setup():
        import jax, jax.numpy as jnp
        import numpy as np
        N_NODES = 6250
        N_EDGES = 62500
        MSG_DIM = 16
        HID_DIM = 16
        N_EDGE_TYPE = 8
        key = jax.random.key(seed)
        ks = jax.random.split(key, 9)
        features = jax.random.normal(ks[0], (N_NODES, HID_DIM), dtype=jnp.float32)
        edge_src = jax.random.randint(ks[1], (N_EDGES,), 0, N_NODES, dtype=jnp.int32)
        edge_dst = jax.random.randint(ks[2], (N_EDGES,), 0, N_NODES, dtype=jnp.int32)
        edge_type = jax.random.randint(ks[3], (N_EDGES,), 0, N_EDGE_TYPE, dtype=jnp.int32)
        edge_emb = jax.random.normal(ks[4], (N_EDGE_TYPE, MSG_DIM * HID_DIM), dtype=jnp.float32) * 0.1
        s = 1.0 / np.sqrt(HID_DIM)
        w_ih = jax.random.uniform(ks[5], (3 * HID_DIM, MSG_DIM), minval=-s, maxval=s, dtype=jnp.float32)
        w_hh = jax.random.uniform(ks[6], (3 * HID_DIM, HID_DIM), minval=-s, maxval=s, dtype=jnp.float32)
        b_ih = jax.random.uniform(ks[7], (3 * HID_DIM,), minval=-s, maxval=s, dtype=jnp.float32)
        b_hh = jax.random.uniform(ks[8], (3 * HID_DIM,), minval=-s, maxval=s, dtype=jnp.float32)
        return {'features': features, 'edge_src': edge_src, 'edge_dst': edge_dst, 'edge_type': edge_type, 'edge_emb': edge_emb, 'w_ih': w_ih, 'w_hh': w_hh, 'b_ih': b_ih, 'b_hh': b_hh}
    _L1_gnn_all = _L1_gnn_setup()
    _L1_gnn_in = {k: v for k, v in _L1_gnn_all.items() if k in ('edge_emb', 'w_ih', 'w_hh', 'b_ih', 'b_hh')}
    del _L1_gnn_all

    def _L2_gnn_setup():
        import jax, jax.numpy as jnp
        import numpy as np
        N_NODES = 62500
        key = jax.random.key(seed)
        k1, k2, k3 = jax.random.split(key, 3)
        x = jax.random.normal(k1, (N_NODES, 16), dtype=jnp.float32)
        edge_index = jax.random.randint(k2, (2, 250000), 0, N_NODES, dtype=jnp.int64)
        W = jax.random.normal(k3, (16, 16), dtype=jnp.float32) * (1.0 / np.sqrt(16.0))
        b = jnp.zeros((16,), dtype=jnp.float32)
        return {'x': x, 'edge_index': edge_index, 'W': W, 'b': b}
    _L2_gnn_all = _L2_gnn_setup()
    _L2_gnn_in = {k: v for k, v in _L2_gnn_all.items() if k in ('W', 'b')}
    del _L2_gnn_all

    def _L3_gnn_setup():
        import jax, jax.numpy as jnp
        import numpy as np
        N, E, IN, OUT, R, B = (3125, 50000, 16, 16, 90, 30)
        key = jax.random.key(seed)
        ks = jax.random.split(key, 9)
        h = jax.random.normal(ks[0], (N, IN), dtype=jnp.float32)
        he = jax.random.normal(ks[1], (E, IN), dtype=jnp.float32)
        Ws = jax.random.normal(ks[2], (OUT, IN), dtype=jnp.float32) * 0.1
        Wa = jax.random.normal(ks[3], (1, 3 * OUT), dtype=jnp.float32) * 0.1
        weight = jax.random.normal(ks[4], (B, IN, OUT), dtype=jnp.float32) * 0.1
        w_comp = jax.random.normal(ks[5], (R, B), dtype=jnp.float32) * 0.1
        src = jax.random.randint(ks[6], (E,), 0, N)
        dst = jax.random.randint(ks[7], (E,), 0, N)
        rel_type = jax.random.randint(ks[8], (E,), 0, R)
        return {'h': h, 'he': he, 'Ws': Ws, 'Wa': Wa, 'weight': weight, 'w_comp': w_comp, 'src': src, 'dst': dst, 'rel_type': rel_type}
    _L3_gnn_all = _L3_gnn_setup()
    _L3_gnn_in = {k: v for k, v in _L3_gnn_all.items() if k in ('Ws', 'Wa', 'weight', 'w_comp')}
    del _L3_gnn_all
    return {'x': x, 'src': src, 'dst': dst, 'edge_attr_16': edge_attr_16, 'edge_type_8': edge_type_8, 'edge_type_90': edge_type_90, 'L0_gnn_enc_W0': _L0_gnn_in['enc_W0'], 'L0_gnn_enc_b0': _L0_gnn_in['enc_b0'], 'L0_gnn_enc_W1': _L0_gnn_in['enc_W1'], 'L0_gnn_enc_b1': _L0_gnn_in['enc_b1'], 'L0_gnn_enc_W2': _L0_gnn_in['enc_W2'], 'L0_gnn_enc_b2': _L0_gnn_in['enc_b2'], 'L0_gnn_lat_W0': _L0_gnn_in['lat_W0'], 'L0_gnn_lat_b0': _L0_gnn_in['lat_b0'], 'L0_gnn_lat_W1': _L0_gnn_in['lat_W1'], 'L0_gnn_lat_b1': _L0_gnn_in['lat_b1'], 'L0_gnn_dfc_W0': _L0_gnn_in['dfc_W0'], 'L0_gnn_dfc_b0': _L0_gnn_in['dfc_b0'], 'L0_gnn_dfc_W1': _L0_gnn_in['dfc_W1'], 'L0_gnn_dfc_b1': _L0_gnn_in['dfc_b1'], 'L0_gnn_dec_W0': _L0_gnn_in['dec_W0'], 'L0_gnn_dec_b0': _L0_gnn_in['dec_b0'], 'L0_gnn_dec_W1': _L0_gnn_in['dec_W1'], 'L0_gnn_dec_b1': _L0_gnn_in['dec_b1'], 'L0_gnn_dec_W2': _L0_gnn_in['dec_W2'], 'L0_gnn_dec_b2': _L0_gnn_in['dec_b2'], 'L1_gnn_edge_emb': _L1_gnn_in['edge_emb'], 'L1_gnn_w_ih': _L1_gnn_in['w_ih'], 'L1_gnn_w_hh': _L1_gnn_in['w_hh'], 'L1_gnn_b_ih': _L1_gnn_in['b_ih'], 'L1_gnn_b_hh': _L1_gnn_in['b_hh'], 'L2_gnn_W': _L2_gnn_in['W'], 'L2_gnn_b': _L2_gnn_in['b'], 'L3_gnn_Ws': _L3_gnn_in['Ws'], 'L3_gnn_Wa': _L3_gnn_in['Wa'], 'L3_gnn_weight': _L3_gnn_in['weight'], 'L3_gnn_w_comp': _L3_gnn_in['w_comp']}

def reference(x, src, dst, edge_attr_16, edge_type_8, edge_type_90, L0_gnn_enc_W0, L0_gnn_enc_b0, L0_gnn_enc_W1, L0_gnn_enc_b1, L0_gnn_enc_W2, L0_gnn_enc_b2, L0_gnn_lat_W0, L0_gnn_lat_b0, L0_gnn_lat_W1, L0_gnn_lat_b1, L0_gnn_dfc_W0, L0_gnn_dfc_b0, L0_gnn_dfc_W1, L0_gnn_dfc_b1, L0_gnn_dec_W0, L0_gnn_dec_b0, L0_gnn_dec_W1, L0_gnn_dec_b1, L0_gnn_dec_W2, L0_gnn_dec_b2, L1_gnn_edge_emb, L1_gnn_w_ih, L1_gnn_w_hh, L1_gnn_b_ih, L1_gnn_b_hh, L2_gnn_W, L2_gnn_b, L3_gnn_Ws, L3_gnn_Wa, L3_gnn_weight, L3_gnn_w_comp):
    import jax
    import jax.numpy as jnp

    def _L0_gnn_ref(x, edge_index, enc_W0, enc_b0, enc_W1, enc_b1, enc_W2, enc_b2, lat_W0, lat_b0, lat_W1, lat_b1, dfc_W0, dfc_b0, dfc_W1, dfc_b1, dec_W0, dec_b0, dec_W1, dec_b1, dec_W2, dec_b2):
        import jax, jax.numpy as jnp
        import numpy as np
        N = 3125
        E = 25000
        IN_CH = 16
        SLOPE = 0.01

        def leaky(v):
            return jnp.where(v > 0, v, SLOPE * v)

        def gcn_conv(x, src, dst, W, b, n):
            h = x @ W
            deg = jnp.zeros((n,), x.dtype).at[dst].add(1.0) + 1.0
            dinv = jax.lax.rsqrt(deg)
            norm = dinv[src] * dinv[dst]
            agg = jax.ops.segment_sum(h[src] * norm[:, None], dst, num_segments=n)
            agg = agg + h * (dinv * dinv)[:, None]
            return agg + b
        src, dst = (edge_index[0], edge_index[1])
        n = x.shape[0]
        h = leaky(gcn_conv(x, src, dst, enc_W0, enc_b0, n))
        h = leaky(gcn_conv(h, src, dst, enc_W1, enc_b1, n))
        h = leaky(gcn_conv(h, src, dst, enc_W2, enc_b2, n))
        h = leaky(h @ lat_W0 + lat_b0)
        h = h @ lat_W1 + lat_b1
        h = leaky(h @ dfc_W0 + dfc_b0)
        h = leaky(h @ dfc_W1 + dfc_b1)
        h = leaky(gcn_conv(h, src, dst, dec_W0, dec_b0, n))
        h = leaky(gcn_conv(h, src, dst, dec_W1, dec_b1, n))
        h = leaky(gcn_conv(h, src, dst, dec_W2, dec_b2, n))
        return jnp.tanh(h)

    def _L1_gnn_ref(features, edge_src, edge_dst, edge_type, edge_emb, w_ih, w_hh, b_ih, b_hh):
        import jax, jax.numpy as jnp
        import numpy as np
        N_NODES = 6250
        N_EDGES = 62500
        MSG_DIM = 16
        HID_DIM = 16
        N_EDGE_TYPE = 8
        n_nodes = features.shape[0]
        A = edge_emb[edge_type].reshape(-1, MSG_DIM, HID_DIM)
        h_src = features[edge_src]
        msg = jnp.einsum('emh,eh->em', A, h_src)
        m = jax.ops.segment_sum(msg, edge_dst, num_segments=n_nodes)
        gi = m @ w_ih.T + b_ih
        gh = features @ w_hh.T + b_hh
        i_r, i_z, i_n = jnp.split(gi, 3, axis=-1)
        h_r, h_z, h_n = jnp.split(gh, 3, axis=-1)
        r = jax.nn.sigmoid(i_r + h_r)
        z = jax.nn.sigmoid(i_z + h_z)
        n = jnp.tanh(i_n + r * h_n)
        h_new = (1.0 - z) * n + z * features
        return h_new

    def _L2_gnn_ref(x, edge_index, W, b):
        import jax, jax.numpy as jnp
        import numpy as np
        N_NODES = 62500
        n = x.shape[0]
        row, col = (edge_index[0], edge_index[1])
        h = x @ W
        deg = jax.ops.segment_sum(jnp.ones_like(col, dtype=h.dtype), col, num_segments=n) + 1.0
        dinv = jax.lax.rsqrt(deg)
        norm = dinv[row] * dinv[col]
        msgs = h[row] * norm[:, None]
        agg = jax.ops.segment_sum(msgs, col, num_segments=n)
        out = agg + h * (dinv * dinv)[:, None] + b
        return out

    def _L3_gnn_ref(h, he, Ws, Wa, weight, w_comp, src, dst, rel_type):
        import jax, jax.numpy as jnp
        import numpy as np
        N, E, IN, OUT, R, B = (3125, 50000, 16, 16, 90, 30)
        n_nodes, in_dim = h.shape
        num_bases, _, out_dim = weight.shape
        num_rels = w_comp.shape[0]
        V = weight.reshape(in_dim, num_bases, out_dim)
        W_rel = jnp.matmul(w_comp, V).reshape(num_rels, in_dim, out_dim)
        h_src = h[src]
        z_src = h_src @ Ws.T
        z_dst = h[dst] @ Ws.T
        z_e = he @ Ws.T
        e = jnp.concatenate([z_src, z_e, z_dst], axis=1) @ Wa.T
        msg = jnp.einsum('ei,eio->eo', h_src, W_rel[rel_type]) * e
        h_out = jax.ops.segment_sum(msg, dst, num_segments=n_nodes)
        return h_out
    edge_index = jnp.stack([src, dst])
    h = jnp.maximum(_layernorm(x, axis=-1), 0.0)
    x = x + _L0_gnn_ref(h, edge_index, L0_gnn_enc_W0, L0_gnn_enc_b0, L0_gnn_enc_W1, L0_gnn_enc_b1, L0_gnn_enc_W2, L0_gnn_enc_b2, L0_gnn_lat_W0, L0_gnn_lat_b0, L0_gnn_lat_W1, L0_gnn_lat_b1, L0_gnn_dfc_W0, L0_gnn_dfc_b0, L0_gnn_dfc_W1, L0_gnn_dfc_b1, L0_gnn_dec_W0, L0_gnn_dec_b0, L0_gnn_dec_W1, L0_gnn_dec_b1, L0_gnn_dec_W2, L0_gnn_dec_b2)
    h = jnp.maximum(_layernorm(x, axis=-1), 0.0)
    x = x + _L1_gnn_ref(h, src, dst, edge_type_8, L1_gnn_edge_emb, L1_gnn_w_ih, L1_gnn_w_hh, L1_gnn_b_ih, L1_gnn_b_hh)
    h = jnp.maximum(_layernorm(x, axis=-1), 0.0)
    x = x + _L2_gnn_ref(h, edge_index, L2_gnn_W, L2_gnn_b)
    h = jnp.maximum(_layernorm(x, axis=-1), 0.0)
    x = x + _L3_gnn_ref(h, edge_attr_16, L3_gnn_Ws, L3_gnn_Wa, L3_gnn_weight, L3_gnn_w_comp, src, dst, edge_type_90)
    return x

_drawn_inputs = setup_inputs


def setup_inputs(seed=0):
    import zlib

    import numpy as np

    out = dict(_drawn_inputs(seed))
    spreads = {'L0_gnn_enc_b0': (0.0, 0.8),
     'L0_gnn_enc_b1': (0.0, 0.8),
     'L0_gnn_enc_b2': (0.0, 2.0),
     'L0_gnn_lat_b0': (0.0, 2.0),
     'L0_gnn_lat_b1': (0.0, 1.204),
     'L0_gnn_dfc_b0': (0.0, 1.157),
     'L0_gnn_dfc_b1': (0.0, 1.253),
     'L0_gnn_dec_b0': (0.0, 0.8),
     'L0_gnn_dec_b1': (0.0, 0.282),
     'L0_gnn_dec_b2': (0.0, 0.8),
     'L2_gnn_b': (0.0, 0.1)}
    factors = {'L0_gnn_enc_W0': 3.242,
     'L0_gnn_enc_W1': 5.829,
     'L0_gnn_lat_W0': 3.206,
     'L1_gnn_b_hh': 2.74}
    for name, (base, spread) in spreads.items():
        noise = np.random.default_rng([zlib.crc32(name.encode()), seed]).standard_normal(out[name].shape)
        drawn = base * np.exp(spread * noise) if base else spread * noise
        out[name] = jnp.asarray(drawn.astype(out[name].dtype))
    for name, factor in factors.items():
        out[name] = (out[name] * factor).astype(out[name].dtype)
    return out
```

```python
import concourse.bass as bass
from concourse import mybir
from contextlib import ExitStack

F32, BF16, I32, U32 = mybir.dt.float32, mybir.dt.bfloat16, mybir.dt.int32, mybir.dt.uint32
ALU = mybir.AluOpType
ACT = mybir.ActivationFunctionType
AX = mybir.AxisListType

P = 128
N, E, F = 6250, 206250, 16
NT = -(-N // P)
NP = NT * P
SUP = 8
BODY = 2 * SUP
ITS = -(-E // (P * BODY))
ET = ITS * BODY
EP = ET * P
SG = ET // SUP
SE = SUP * P
SHIFT = 13
ROW = 1 << SHIFT
R8, R90 = 8, 90
MANY = 1024
BITS = 16
CH = 448
HALF = 7
RING = 7
TG = 7
EPS = 1e-5
SLOPE = 0.01



class Counted:

    def __init__(self, nc, name):
        self.sem = nc.alloc_semaphore(name)
        self.n = 0

    def by(self, ins, k=1):
        ins.then_inc(self.sem, k)
        self.n += k
        return (self.sem, self.n)


class Looped:

    def __init__(self, nc, name, per=1, step=1):
        self.sem, self.per, self.step, self.n0 = nc.alloc_semaphore(name), per, step, 0

    def credit(self, eng, depth):
        eng.sem_inc(self.sem, depth * self.step)
        self.n0 += depth * self.step

    def credit_dma(self, ins):
        ins.then_inc(self.sem, self.step)
        self.n0 += self.step

    def at(self, it, k):
        return it * (self.per * self.step) + (self.n0 + k * self.step)

    def close(self, its):
        self.n0 += its * self.per * self.step
        return (self.sem, self.n0)


def need(eng, *tokens):
    for sem, value in tokens:
        eng.wait_ge(sem, value)


def program(nc, t, wcols, out):
    pe, dve, act, pool, sp = nc.tensor, nc.vector, nc.scalar, nc.gpsimd, nc.sync
    engines = [pe.engine, dve.engine, act.engine, pool.engine, sp.engine]
    life = ExitStack()

    turns = nc.alloc_semaphore("turns")

    def hold(eng, sem, value):
        eng.wait_ge(sem, value)
        eng.sem_inc(turns, 1)

    done = {e: Counted(nc, f"done_{n}") for e, n in ((pe, "pe"), (dve, "dve"), (act, "act"), (pool, "pool"))}
    s_load = Counted(nc, "loaded")

    def step(eng, ins):
        return done[eng].by(ins)

    def link(eng, ins):
        tok = step(eng, ins)
        need(eng, tok)
        return tok

    def sb(stack, name, shape, dt=F32):
        return stack.enter_context(nc.sbuf_tensor(name, list(shape), dt))

    def banks(stack, name, n):
        return [stack.enter_context(nc.psum_tensor(f"{name}{b}", [P, 512], F32)) for b in range(n)]

    adj = nc.dram_tensor("adj", (NP * ROW, 1), BF16).ap()
    adj_rows = adj.rearrange("(r c) o -> r (c o)", c=ROW)
    h_dram = nc.dram_tensor("h_rows", (NP, F), F32).ap()
    m1_dram = nc.dram_tensor("m1_rows", (NP + P, F), F32).ap()
    m3_dram = nc.dram_tensor("m3_rows", (NP + P, 2 * F), F32).ap()
    dinv_dram = nc.dram_tensor("dinv_row", (NT, P), F32).ap()
    rel_dram = nc.dram_tensor("rel_flat", (F, R90, F), F32).ap()

    X = sb(life, "X", [P, NT, F])
    W = sb(life, "W", [P, t["wpack"].shape[1]])
    I128 = sb(life, "I128", [P, P])
    dloc = sb(life, "dloc", [P, ET])
    rowI = sb(life, "rowI", [P, SG], I32)
    dinvN = sb(life, "dinvN", [P, NT])
    iotaP = sb(life, "iotaP", [P, 1])
    iotaPi = sb(life, "iotaPi", [P, 1], I32)
    iota128 = sb(life, "iota128", [P, P])
    bitno = sb(life, "bitno", [2 * BITS, 1], I32)
    H = sb(life, "H", [P, NT, F])
    q1 = sb(life, "q1", [P, NT, F])
    mean = sb(life, "mean", [P, NT])
    var = sb(life, "var", [P, NT])

    def w(name):
        r, c0, c1 = wcols[name]
        return W[0:r, c0:c1]

    def over(ap, n):
        return ap.rearrange("p (a o) -> p a o", o=1).to_broadcast([ap.shape[0], ap.shape[1], n])

    def under(ap, n):
        return ap.rearrange("p (o a) -> p o a", o=1).to_broadcast([ap.shape[0], n, ap.shape[1]])

    def norm(x_tok):
        need(dve, x_tok)
        link(dve, dve.tensor_reduce(mean[:, :], X[:, :, :], AX.X, ALU.add))
        link(dve, dve.tensor_scalar(mean[:, :], mean[:, :], 1.0 / F, None, ALU.mult))
        link(dve, dve.tensor_tensor(H[:, :, :], X[:, :, :], over(mean[:, :], F), ALU.subtract))
        link(dve, dve.tensor_tensor(q1[:, :, :], H[:, :, :], H[:, :, :], ALU.mult))
        link(dve, dve.tensor_reduce(var[:, :], q1[:, :, :], AX.X, ALU.add))
        need(act, link(dve, dve.tensor_scalar(var[:, :], var[:, :], 1.0 / F, EPS, ALU.mult, ALU.add)))
        need(dve, step(act, act.activation(var[:, :], var[:, :], ACT.Sqrt)))
        link(dve, dve.reciprocal(var[:, :], var[:, :]))
        link(dve, dve.tensor_tensor(H[:, :, :], H[:, :, :], over(var[:, :], F), ALU.mult))
        return link(dve, dve.tensor_scalar(H[:, :, :], H[:, :, :], 0.0, None, ALU.max))

    setup = ExitStack()
    dstI = sb(setup, "dstI", [P, ET], I32)
    srcI = sb(setup, "srcI", [P, ET], I32)
    baseI = sb(setup, "baseI", [P, SG], I32)
    iotaH = sb(setup, "iotaH", [P, P], I32)
    zrow = sb(setup, "zrow", [P, NP], BF16)
    ones = sb(setup, "ones", [P, NT], BF16)
    link(dve, dve.memset(zrow[:, :], 0.0))
    need(sp, link(dve, dve.memset(ones[:, :], 1.0)))

    def load(dst, src):
        return s_load.by(sp.dma_start(dst, src), 16)

    load(dstI[:, :], t["dst_pm"])
    load(srcI[:, :], t["src_pm"])
    load(baseI[:, :], t["dst_base"].to_broadcast([P, SG]))
    load(X[:, :, :], t["x"].rearrange("(t p) f -> p t f", p=P))
    loaded = load(W[:, :], t["wpack"])
    step(pool, pool.iota(iotaPi[:, :], pattern=[[0, 1]], base=0, channel_multiplier=1))
    step(pool, pool.iota(iota128[:, :], pattern=[[1, P]], base=0, channel_multiplier=0, allow_small_or_imprecise_dtypes=True))
    step(pool, pool.iota(iotaH[:, :], pattern=[[1, P]], base=0, channel_multiplier=0))
    link(pool, pool.memset(I128[:, :], 0.0))
    ready = step(pool, pool.affine_select(out=I128[:, :], in_=I128[:, :], compare_op=ALU.not_equal, fill=1.0,
                                          base=0, pattern=[[-1, P]], channel_multiplier=1))
    s_zero = Counted(nc, "zeroed")
    for k in range(NT):
        zeroed = s_zero.by(sp.dma_start(adj_rows[k * P:(k + 1) * P, 0:NP], zrow[:, :]), 16)
    zf = zrow[:, :].bitcast(F32)
    MT = (NP + P) // P
    s_sums = Counted(nc, "sums_zeroed")
    s_sums.by(sp.dma_start(m1_dram.rearrange("(p m) c -> p (m c)", p=P), zf[:, 0:MT * F]), 16)
    s_sums.by(sp.dma_start(m3_dram.rearrange("(p m) c -> p (m c)", p=P), zf[:, 0:2 * MT * F]), 16)
    need(sp, zeroed)
    s_diag = Counted(nc, "diagonal_set")
    with nc.allow_non_contiguous_dma(reason="the diagonal's cells"):
        for k in range(NT):
            cells = bass.AP(tensor=adj.tensor, offset=k * P * (ROW + 1), ap=[[ROW + 1, P], [1, 1]])
            diagonal = s_diag.by(sp.dma_start(cells, ones[:, k:k + 1]), 16)

    need(dve, loaded, ready)
    step(dve, dve.tensor_copy(iotaP[:, :], iotaPi[:, :]))
    step(dve, dve.tensor_scalar(bitno[:, :], iotaPi[0:2 * BITS, :], BITS - 1, None, ALU.bitwise_and))
    step(dve, dve.tensor_tensor(dloc[:, :].rearrange("p (s e) -> p s e", e=SUP),
                                dstI[:, :].rearrange("p (s e) -> p s e", e=SUP), over(baseI[:, :], SUP), ALU.subtract))
    link(dve, dve.tensor_tensor(rowI[:, :], baseI[:, :], iotaPi[:, :].to_broadcast([P, SG]), ALU.add))
    h_tok = norm(loaded)

    build = ExitStack()
    WIN = SE + 2 * P
    keyrow = [sb(build, f"keyrow{h}", [2 * BITS, WIN], I32) for h in range(2)]
    keybit = [sb(build, f"keybit{h}", [2 * BITS, WIN], I32) for h in range(2)]
    keypm = [sb(build, f"keypm{h}", [2 * BITS, WIN], BF16) for h in range(2)]
    hit = sb(build, "hit", [P, 4, 3 * P], BF16)
    cnt = [sb(build, f"cnt{h}", [P, SUP]) for h in range(2)]
    same = [sb(build, f"same{h}", [P, SUP]) for h in range(2)]
    val = [sb(build, f"val{h}", [P, SUP], BF16) for h in range(2)]
    cell = [sb(build, f"cell{h}", [P, SUP], U32) for h in range(2)]
    later = [sb(build, f"later{h}", [P, SUP], I32) for h in range(2)]
    away = [sb(build, f"away{h}", [P, SUP], I32) for h in range(2)]
    spare = sb(build, "spare", [P, ET], I32)
    rank = sb(build, "rank", [P, 3 * P])
    dlo = sb(build, "dlo", [P, ET], I32)
    dhi = sb(build, "dhi", [P, ET], I32)
    ohlo = [sb(build, f"ohlo{h}", [P, SUP, P], BF16) for h in range(2)]
    ohhi = [sb(build, f"ohhi{h}", [P, SUP, NT], BF16) for h in range(2)]
    NDOT = 4
    dot = banks(build, "dot", NDOT)
    hist = build.enter_context(nc.psum_tensor("hist", [P, 512], F32))
    assert NP + ET <= ROW and MANY > 3 * P
    step(pool, pool.iota(spare[:, :], pattern=[[1, ET]], base=NP, channel_multiplier=ROW))
    step(pool, pool.memset(rank[:, 0:P], float(MANY)))
    link(pool, pool.memset(rank[:, P:2 * P], float(MANY + 1)))
    step(pool, pool.memset(rank[:, 2 * P:3 * P], 1.0))
    need(dve, step(pool, pool.affine_select(out=rank[:, P:2 * P], in_=rank[:, P:2 * P], compare_op=ALU.is_gt, fill=1.0,
                                            base=0, pattern=[[-1, P]], channel_multiplier=1)))
    step(dve, dve.tensor_scalar(dlo[:, :], dstI[:, :], P - 1, None, ALU.bitwise_and))
    cols = link(dve, dve.tensor_scalar(dhi[:, :], dstI[:, :], 7, None, ALU.logical_shift_right))

    b_row = [Looped(nc, f"b_row{h}", 2, 16) for h in range(2)]
    b_bit = Looped(nc, "b_bit", 2)
    b_pm = Looped(nc, "b_pm", 2)
    b_oh = Looped(nc, "b_oh", 2)
    b_dot = Looped(nc, "b_dot", BODY)
    b_mm = Looped(nc, "b_mm", 2)
    b_cnt = Looped(nc, "b_cnt", BODY)
    b_key = Looped(nc, "b_key", 2 * 7)
    b_val = Looped(nc, "b_val", 2)
    b_sc = [Looped(nc, f"b_sc{h}", SUP, 16) for h in range(2)]
    b_bit.credit(dve, 2)
    b_pm.credit(act, 2)
    b_mm.credit(pe, 2)
    b_cnt.credit(dve, NDOT)
    for h in range(2):
        b_sc[h].credit_dma(pool.dma_start(cell[h][:, :], t["src_pm"][:, 0:SUP].bitcast(U32)))
    need(pe, cols)
    step(pe, pe.matmul(hist[:, 0:NT], zrow[:, 0:P], zrow[:, 0:NT], start=True, stop=False, skip_group_check=True))
    need(pool, diagonal)
    need(dve, cols)
    with nc.Fori(0, ITS, engines=engines) as it:
        for h in range(2):
            k = 2 * it + h
            sp.wait_ge(b_bit.sem, b_bit.at(it, h - 1))
            win = bass.ds(k * SE, WIN)
            sp.dma_start(keyrow[h][0:BITS, :], t["src_row"][:, win].to_broadcast([BITS, WIN])).then_inc(b_row[h].sem, 16)
            sp.dma_start(keyrow[h][BITS:2 * BITS, :], t["dst_row"][:, win].to_broadcast([BITS, WIN])).then_inc(b_row[h].sem, 16)
            dve.wait_ge(b_pm.sem, b_pm.at(it, h - 1))
            dve.wait_ge(b_row[h].sem, b_row[h].at(it, 2))
            dve.tensor_scalar(keybit[h][:, :], keyrow[h][:, :], bitno[:, 0:1], 1,
                              ALU.logical_shift_right, ALU.bitwise_and).then_inc(b_bit.sem, 1)
            act.wait_ge(b_mm.sem, b_mm.at(it, h - 1))
            act.wait_ge(b_bit.sem, b_bit.at(it, h + 1))
            act.activation(keypm[h][:, :], keybit[h][:, :], ACT.Copy, bias=-1.0, scale=2.0).then_inc(b_pm.sem, 1)
            dve.wait_ge(b_mm.sem, b_mm.at(it, h - 1))
            e8 = bass.ds(k * SUP, SUP)
            dve.tensor_tensor(ohlo[h][:, :, :], under(iotaH[:, :], SUP), over(dlo[:, e8], P), ALU.is_equal)
            dve.tensor_tensor(ohhi[h][:, :, :], under(iotaH[:, 0:NT], SUP), over(dhi[:, e8], NT),
                              ALU.is_equal).then_inc(b_oh.sem, 1)
            hold(pe, b_pm.sem, b_pm.at(it, h + 1))
            for j in range(SUP):
                i = h * SUP + j
                hold(pe, b_cnt.sem, b_cnt.at(it, i + 1 - NDOT))
                pe.matmul(dot[j % NDOT][:, 0:3 * P], keypm[h][:, (j + 1) * P:(j + 2) * P], keypm[h][:, j * P:(j + 3) * P],
                          start=True, stop=True).then_inc(b_dot.sem, 1)
            hold(pe, b_oh.sem, b_oh.at(it, h + 1))
            for j in range(SUP):
                ins = pe.matmul(hist[:, 0:NT], ohlo[h][:, j, :], ohhi[h][:, j, :], start=False, stop=False,
                                skip_group_check=True)
            ins.then_inc(b_mm.sem, 1)
            dve.wait_ge(b_sc[h].sem, b_sc[h].at(it, 0))
            for j in range(SUP):
                i = h * SUP + j
                dve.wait_ge(b_dot.sem, b_dot.at(it, i + 1))
                dve.scalar_tensor_tensor(hit[:, j % 4, :], dot[j % NDOT][:, 0:3 * P], float(2 * BITS), rank[:, :],
                                         ALU.is_equal, ALU.mult, accum_out=cnt[h][:, j:j + 1]).then_inc(b_cnt.sem, 1)
            dve.tensor_tensor(same[h][:, :], srcI[:, e8], dstI[:, e8], ALU.is_equal).then_inc(b_key.sem, 1)
            dve.tensor_scalar(cell[h][:, :].bitcast(I32), srcI[:, e8], SHIFT, None, ALU.logical_shift_left).then_inc(b_key.sem, 1)
            dve.wait_ge(b_cnt.sem, b_cnt.at(it, (h + 1) * SUP))
            dve.wait_ge(b_key.sem, b_key.at(it, 7 * h + 2))
            c8 = cell[h][:, :].bitcast(I32)
            dve.tensor_tensor(val[h][:, :], cnt[h][:, :], same[h][:, :], ALU.add).then_inc(b_key.sem, 1)
            dve.tensor_tensor(c8, c8, dstI[:, e8], ALU.bitwise_or).then_inc(b_key.sem, 1)
            dve.tensor_scalar(later[h][:, :], cnt[h][:, :], float(MANY), -1.0, ALU.is_ge, ALU.mult).then_inc(b_key.sem, 1)
            dve.wait_ge(b_key.sem, b_key.at(it, 7 * h + 5))
            dve.tensor_tensor(away[h][:, :], later[h][:, :], spare[:, e8], ALU.bitwise_and).then_inc(b_key.sem, 1)
            dve.scalar_tensor_tensor(c8, later[h][:, :], -1, c8, ALU.bitwise_xor, ALU.bitwise_and).then_inc(b_key.sem, 1)
            dve.wait_ge(b_key.sem, b_key.at(it, 7 * h + 7))
            dve.tensor_tensor(c8, c8, away[h][:, :], ALU.bitwise_or).then_inc(b_val.sem, 1)
            hold(pool, b_val.sem, b_val.at(it, h + 1))
            for j in range(SUP):
                pool.indirect_dma_start(adj, bass.IndirectOffsetOnAxis(ap=cell[h][:, j:j + 1], axis=0),
                                        val[h][:, j:j + 1], None).then_inc(b_sc[h].sem, 16)
    scattered = [s.close(ITS) for s in b_sc]
    counted = b_mm.close(ITS)
    need(dve, counted)
    link(dve, dve.tensor_scalar(dinvN[:, :], hist[:, 0:NT], 1.0, None, ALU.add))
    need(act, (done[dve].sem, done[dve].n))
    need(dve, step(act, act.activation(dinvN[:, :], dinvN[:, :], ACT.Sqrt)))
    need(pe, link(dve, dve.reciprocal(dinvN[:, :], dinvN[:, :])))
    need(dve, step(pe, pe.transpose(dot[0][0:NT, 0:P], dinvN[:, :], I128[:, :])))
    dinvT = sb(build, "dinvT", [NT, P])
    need(sp, step(dve, dve.tensor_copy(dinvT[:, :], dot[0][0:NT, 0:P])))
    need(sp, s_load.by(sp.dma_start(dinv_dram, dinvT[:, :]), 16))
    need(sp, *scattered)
    need(sp, (s_sums.sem, s_sums.n))
    nc.all_engine_barrier()
    build.close()
    setup.close()

    def dense_scope(name):
        s = ExitStack()
        d = dict(
            ring=[sb(s, f"{name}_ring{j}", [P, HALF * CH], BF16) for j in range(RING)],
            Y=sb(s, f"{name}_Y", [P, NP]),
            T=sb(s, f"{name}_T", [P, NT, 3 * 64], BF16),
            tmp=sb(s, f"{name}_tmp", [P, NT, 64]),
            dinvB=sb(s, f"{name}_dinvB", [P, NP]),
            ps=banks(s, f"{name}_ps", 8),
            s_in=[Counted(nc, f"{name}_in{j}") for j in range(RING)],
            s_row=Counted(nc, f"{name}_row"),
            free={},
            stack=s)
        s_d = Counted(nc, f"{name}_dinv")
        flat = dinv_dram.rearrange("(o t) p -> o (t p)", o=1)
        d["dinv_tok"] = s_d.by(act.dma_start(d["dinvB"][:, :], flat.to_broadcast([P, NP])), 16)
        return d

    def split_table(d, Fo, sources, free):
        T, tmp = d["T"], d["tmp"]
        need(dve, *free)
        need(act, *free)
        scaled, hi, rest, mid = [], [], [], []
        groups = range(NT // TG)

        def part(g, p):
            return T[:, g * TG:(g + 1) * TG, p * Fo:(p + 1) * Fo]

        def tm(g):
            return tmp[:, g * TG:(g + 1) * TG, 0:Fo]

        for g in groups:
            src, toks = sources(g)
            need(dve, *toks)
            scaled.append(step(dve, dve.tensor_tensor(tm(g), src, over(dinvN[:, g * TG:(g + 1) * TG], Fo), ALU.mult)))
        for g in groups:
            need(act, scaled[g])
            hi.append(step(act, act.activation(part(g, 0), tm(g), ACT.Copy)))
        for g in groups:
            need(dve, hi[g])
            rest.append(step(dve, dve.tensor_tensor(tm(g), tm(g), part(g, 0), ALU.subtract)))
        for g in groups:
            need(act, rest[g])
            mid.append(step(act, act.activation(part(g, 1), tm(g), ACT.Copy)))
        for g in groups:
            need(dve, mid[g])
            last = step(dve, dve.tensor_tensor(part(g, 2), tm(g), part(g, 1), ALU.subtract))
        return scaled, last

    def aggregate(d, Fo, table_toks):
        rows = 128 if Fo == 64 else 48
        T, ring, ps, s_in, s_row = d["T"], d["ring"], d["ps"], d["s_in"], d["s_row"]
        out = []
        need(pe, *table_toks, *d["free"].values())
        evac = []
        for half in range(2):
            col = half * HALF * CH

            def load_row(j, row_ap):
                return sp.dma_start(ring[j][:, :], row_ap)

            def products(k, j, first):
                for c in range(HALF):
                    a = ring[j][:, c * CH:(c + 1) * CH]
                    ins = pe.matmul(ps[c][0:rows, 0:CH], T[:, k, 0:rows], a, start=first, stop=False, skip_group_check=True)
                if Fo == 64:
                    for c in range(HALF):
                        a = ring[j][:, c * CH:(c + 1) * CH]
                        ins = pe.matmul(ps[c][0:64, 0:CH], T[:, k, 128:192], a, start=False, stop=False, skip_group_check=True)
                return ins

            for j in range(RING):
                if s_row.n:
                    need(sp, (s_row.sem, s_row.n - RING + j + 1))
                s_in[j].by(load_row(j, adj_rows[j * P:(j + 1) * P, col:col + HALF * CH]), 16)
            in0 = [s.n for s in s_in]
            row0 = s_row.n
            for e in evac:
                need(pe, e)
            for j in range(RING):
                need(pe, (s_in[j].sem, s_in[j].n))
                s_row.by(products(j, j, j == 0))
            with nc.Fori(1, NT // RING, engines=[pe.engine, sp.engine]) as it:
                for j in range(RING):
                    sp.wait_ge(s_row.sem, it * RING + (row0 - RING + j + 1))
                    load_row(j, adj_rows[bass.ds(it * (RING * P) + j * P, P), col:col + HALF * CH]).then_inc(s_in[j].sem, 16)
                for j in range(RING):
                    hold(pe, s_in[j].sem, it * 16 + in0[j])
                    for c in range(HALF):
                        a = ring[j][:, c * CH:(c + 1) * CH]
                        ins = pe.matmul(ps[c][0:rows, 0:CH], Tk(T, it * RING + j, 0, rows), a, start=False, stop=False, skip_group_check=True)
                    if Fo == 64:
                        for c in range(HALF):
                            a = ring[j][:, c * CH:(c + 1) * CH]
                            ins = pe.matmul(ps[c][0:64, 0:CH], Tk(T, it * RING + j, 128, 192), a, start=False, stop=False, skip_group_check=True)
                    ins.then_inc(s_row.sem, 1)
            for j in range(RING):
                s_in[j].n += 16 * (NT // RING - 1)
            s_row.n += RING * (NT // RING - 1)
            need(dve, (s_row.sem, s_row.n), d["dinv_tok"])
            evac = []
            for c in range(HALF):
                cc = slice(col + c * CH, col + (c + 1) * CH)
                d["free"][c] = (done[dve].sem, done[dve].n + 1)
                evac.append(step(dve, dve.tensor_tensor(d["Y"][0:rows, cc], ps[c][0:rows, 0:CH], d["dinvB"][0:rows, cc], ALU.mult)))
            out += evac
        return rows, out

    def bank_free(d, b):
        return [d["free"][b]] if b in d["free"] else []

    def Tk(T, k, a, b):
        return T[:, bass.ds(k, 1), a:b].rearrange("p o c -> p (o c)")

    def feature_layer(d, name, rows, Fo, toks, bias, leaky=True):
        Y, ps = d["Y"], d["ps"]
        outs = []
        for c in range(2 * HALF):
            cc = slice(c * CH, (c + 1) * CH)
            bank = ps[c % 8]
            need(pe, toks[c], *bank_free(d, c % 8))
            need(act, step(pe, pe.matmul(bank[0:Fo, 0:CH], w(name), Y[0:rows, cc], start=True, stop=True)))
            outs.append(step(act, act.activation(Y[0:Fo, cc], bank[0:Fo, 0:CH], ACT.Identity, bias=w(bias))))
            d["free"][c % 8] = outs[-1]
            if leaky:
                need(dve, outs[-1])
                outs[-1] = step(dve, dve.scalar_tensor_tensor(Y[0:Fo, cc], Y[0:Fo, cc], SLOPE, Y[0:Fo, cc], ALU.mult, ALU.max))
        return outs

    def table_from_Y(d, name, Fi, Fo, toks):
        ps = d["ps"]
        free = list(toks)
        tks = {}

        def sources(g):
            bank = ps[g]
            need(pe, *toks, *bank_free(d, g))
            d["free"][g] = (done[dve].sem, done[dve].n + 1)
            for i in range(TG):
                n = (g * TG + i) * P
                tok = pe.matmul(bank[:, i * Fo:(i + 1) * Fo], d["Y"][0:Fi, n:n + P], w(name), start=True, stop=True)
            tok = step(pe, tok)
            return bank[:, 0:TG * Fo].rearrange("p (t f) -> p t f", f=Fo), [tok]

        _, last = split_table(d, Fo, sources, free)
        return [last]

    def to_nodes(d, toks, extra=None):
        ps = d["ps"]
        need(pe, *toks)
        per = 512 // F
        outs = []
        for b in range(0, NT, per):
            m = min(per, NT - b)
            bank = ps[b // per]
            need(pe, *bank_free(d, b // per))
            for i in range(m):
                n = (b + i) * P
                ins = pe.transpose(bank[:, i * F:(i + 1) * F], d["Y"][0:F, n:n + P], I128[0:F, 0:F])
            need(dve, step(pe, ins))
            src = bank[:, 0:m * F].rearrange("p (t f) -> p t f", f=F)
            outs.append(link(dve, dve.tensor_tensor(X[:, b:b + m, :], X[:, b:b + m, :], src, ALU.add)))
        return outs[-1]

    def to_features(d, src, Fi, toks):
        outs = []
        need(pe, *toks)
        for b in range(0, NT, 4):
            m = min(4, NT - b)
            bank = d["ps"][(b // 4) % 8]
            need(pe, *bank_free(d, (b // 4) % 8))
            for i in range(m):
                ins = pe.transpose(bank[0:Fi, i * P:(i + 1) * P], src[:, b + i, :], I128[:, :])
            need(dve, step(pe, ins))
            outs.append(step(dve, dve.tensor_copy(d["Y"][0:Fi, b * P:(b + m) * P], bank[0:Fi, 0:m * P])))
            d["free"][(b // 4) % 8] = outs[-1]
        return outs

    def chunkwise(toks):
        return [toks[-1]] * (2 * HALF)

    d = dense_scope("L0")
    tmp = d["tmp"]
    _, last = split_table(d, F, lambda g: (H[:, g * TG:(g + 1) * TG, :], []), [h_tok])
    rows, y = aggregate(d, F, [last])
    y = feature_layer(d, "enc0", rows, 64, y, "enc_b0")
    rows, y = aggregate(d, 64, table_from_Y(d, "eye64", 64, 64, y))
    y = feature_layer(d, "enc1", rows, 128, y, "enc_b1")
    rows, y = aggregate(d, 64, table_from_Y(d, "enc2", 128, 64, y))
    y = feature_layer(d, "fold64", rows, 64, y, "enc_b2")
    y = feature_layer(d, "lat0", 64, 32, y, "lat_b0")
    y = feature_layer(d, "lat1", 32, 3, y, "lat_b1", leaky=False)
    y = feature_layer(d, "dfc0", 3, 32, y, "dfc_b0")
    y = feature_layer(d, "dfc1", 32, 64, y, "dfc_b1")
    rows, y = aggregate(d, 64, table_from_Y(d, "eye64", 64, 64, y))
    y = feature_layer(d, "dec0", rows, 128, y, "dec_b0")
    rows, y = aggregate(d, 64, table_from_Y(d, "dec1", 128, 64, y))
    y = feature_layer(d, "fold64", rows, 64, y, "dec_b1")
    rows, y = aggregate(d, F, table_from_Y(d, "dec2", 64, F, y))
    y = feature_layer(d, "fold16", rows, F, y, "dec_b2")
    need(act, *y)
    for half in range(2):
        hs = slice(half * HALF * CH, (half + 1) * HALF * CH)
        y.append(step(act, act.activation(d["Y"][0:F, hs], d["Y"][0:F, hs], ACT.Tanh)))
    x_tok = to_nodes(d, y[-2:])
    nc.all_engine_barrier()
    d["stack"].close()

    def edge_layer(name, R, C, types, table, m_dram, attr=None):
        s = ExitStack()
        g = [sb(s, f"{name}_g{h}", [P, SUP, F]) for h in range(2)]
        gidx = [sb(s, f"{name}_gi{h}", [P, SUP], U32) for h in range(2)]
        ridx = [sb(s, f"{name}_ri{h}", [P, 1], U32) for h in range(2)]
        trow = [sb(s, f"{name}_tr{h}", [R, SE], I32) for h in range(2)]
        oht = [sb(s, f"{name}_ot{h}", [R, SE], BF16) for h in range(2)]
        ohw = [sb(s, f"{name}_ow{h}", [P, SUP, P]) for h in range(2)]
        prod = [sb(s, f"{name}_pr{b}", [P, 2, F, F]) for b in range(2)]
        msg = [sb(s, f"{name}_ms{h}", [P, SUP, C]) for h in range(2)]
        sums = [sb(s, f"{name}_su{h}", [P, C]) for h in range(2)]
        psw = banks(s, f"{name}_w", 4)
        psa = banks(s, f"{name}_a", 2)
        if attr is not None:
            he = [sb(s, f"{name}_he{h}", [P, SUP, F]) for h in range(2)]
            ea = [sb(s, f"{name}_ea{h}", [P, SUP, F]) for h in range(2)]
            eb = [sb(s, f"{name}_eb{h}", [P, SUP, F]) for h in range(2)]
            e_ = [sb(s, f"{name}_e{h}", [P, SUP]) for h in range(2)]
        L = lambda n, per=2, st=1: Looped(nc, f"{name}_{n}", per, st)
        e_idx = [L(f"idx{h}", 1, 16) for h in range(2)]
        e_row = [L(f"row{h}", 1 if attr is None else 2, 16) for h in range(2)]
        e_g = [L(f"g{h}", SUP, 16) for h in range(2)]
        e_add = [L(f"add{h}", 1, 16) for h in range(2)]
        e_ot = L("ot")
        e_ow = L("ow")
        e_w = L("w", BODY // 2)
        e_pr = L("pr", BODY // 2)
        e_ms = L("ms", BODY // 2)
        e_e = L("e", 10)
        e_fin = L("fin")
        e_acc = L("acc")
        e_su = L("su")
        for x, eng, depth in ((e_ot, dve, 2), (e_fin, dve, 2), (e_pr, dve, 4), (e_ms, dve, 4), (e_acc, pe, 2), (e_su, act, 2)):
            x.credit(eng, depth)
        for h in range(2):
            step(dve, dve.memset(sums[h][:, :], 0.0))
            tok = step(dve, dve.tensor_copy(ridx[h][:, :].bitcast(I32), rowI[:, 0:1]))
            e_g[h].credit_dma(pool.dma_start(g[h][:, 0, :], h_dram[0:P, :]))
        need(pool, tok)
        for h in range(2):
            if h:
                need(pool, (e_add[0].sem, 16))
            e_add[h].credit_dma(pool.indirect_dma_start(m_dram, bass.IndirectOffsetOnAxis(ap=ridx[h][:, 0:1], axis=0),
                                                       sums[h][:, :], None, compute_op=ALU.add))
        with nc.Fori(0, ITS, engines=engines) as it:
            for h in range(2):
                k = 2 * it + h
                sp.wait_ge(e_g[h].sem, e_g[h].at(it, 0))
                sp.dma_start(gidx[h][:, :], t["src_pm"][:, bass.ds(k * SUP, SUP)].bitcast(U32)).then_inc(e_idx[h].sem, 16)
                sp.wait_ge(e_ot.sem, e_ot.at(it, h - 1))
                sp.dma_start(trow[h][:, :], types[:, bass.ds(k * SE, SE)].to_broadcast([R, SE])).then_inc(e_row[h].sem, 16)
                if attr is not None:
                    sp.wait_ge(e_fin.sem, e_fin.at(it, h - 1))
                    sp.dma_start(he[h][:, :, :].rearrange("p e f -> p (e f)"),
                                 attr[bass.ds(k, 1), :, :].rearrange("o p c -> p (o c)")).then_inc(e_row[h].sem, 16)
                hold(pool, e_idx[h].sem, e_idx[h].at(it, 1))
                hold(pool, e_fin.sem, e_fin.at(it, h - 1))
                for j in range(SUP):
                    pool.indirect_dma_start(g[h][:, j, :], None, h_dram, bass.IndirectOffsetOnAxis(ap=gidx[h][:, j:j + 1], axis=0)).then_inc(e_g[h].sem, 16)
                hold(pool, e_su.sem, e_su.at(it, h - 1))
                hold(pool, e_add[1 - h].sem, e_add[1 - h].at(it, h))
                pool.indirect_dma_start(m_dram, bass.IndirectOffsetOnAxis(ap=ridx[h][:, 0:1], axis=0),
                                        sums[h][:, :], None, compute_op=ALU.add).then_inc(e_add[h].sem, 16)
                dve.wait_ge(e_row[h].sem, e_row[h].at(it, 2 if attr is not None else 1))
                dve.wait_ge(e_acc.sem, e_acc.at(it, h - 1))
                dve.tensor_scalar(oht[h][:, :], trow[h][:, :], iotaP[0:R, :], None, ALU.is_equal).then_inc(e_ot.sem, 1)
                dve.tensor_tensor(ohw[h][:, :, :], under(iota128[:, :], SUP), over(dloc[:, bass.ds(k * SUP, SUP)], P), ALU.is_equal).then_inc(e_ow.sem, 1)
                dve.wait_ge(e_g[h].sem, e_g[h].at(it, SUP))
                for q in range(SUP // 2):
                    i = h * (SUP // 2) + q
                    dve.wait_ge(e_w.sem, e_w.at(it, i + 1))
                    dve.wait_ge(e_ms.sem, e_ms.at(it, i + 1 - 2))
                    wq = psw[q][:, :].rearrange("p (t o i) -> p t o i", t=2, o=F)
                    gq = g[h][:, 2 * q:2 * q + 2, :].rearrange("p t (z i) -> p t z i", z=1).to_broadcast([P, 2, F, F])
                    dve.tensor_tensor(prod[q % 2][:, :, :, :], wq, gq, ALU.mult).then_inc(e_pr.sem, 1)
                    dve.wait_ge(e_pr.sem, e_pr.at(it, i + 1))
                    dve.tensor_reduce(msg[h][:, 2 * q:2 * q + 2, C - F:C], prod[q % 2][:, :, :, :], AX.X, ALU.add).then_inc(e_ms.sem, 1)
                if attr is not None:
                    def ue(i):
                        return e_e.at(it, 5 * h + i)
                    u = t_u[:, :]
                    dve.tensor_tensor(ea[h][:, :, :], g[h][:, :, :], under(u[:, 0:F], SUP), ALU.mult).then_inc(e_e.sem, 1)
                    dve.tensor_tensor(eb[h][:, :, :], he[h][:, :, :], under(u[:, F:2 * F], SUP), ALU.mult).then_inc(e_e.sem, 1)
                    dve.wait_ge(e_e.sem, ue(2))
                    dve.tensor_tensor(ea[h][:, :, :], ea[h][:, :, :], eb[h][:, :, :], ALU.add).then_inc(e_e.sem, 1)
                    dve.wait_ge(e_e.sem, ue(3))
                    dve.tensor_reduce(e_[h][:, :], ea[h][:, :, :], AX.X, ALU.add).then_inc(e_e.sem, 1)
                    dve.wait_ge(e_e.sem, ue(4))
                    dve.wait_ge(e_ms.sem, e_ms.at(it, (h + 1) * SUP // 2))
                    dve.tensor_tensor(msg[h][:, :, 0:F], msg[h][:, :, F:C], over(e_[h][:, :], F), ALU.mult).then_inc(e_e.sem, 1)
                    dve.wait_ge(e_e.sem, ue(5))
                else:
                    dve.wait_ge(e_ms.sem, e_ms.at(it, (h + 1) * SUP // 2))
                dve.wait_ge(e_add[h].sem, e_add[h].at(it, 1))
                dve.tensor_copy(ridx[h][:, :].bitcast(I32), rowI[:, bass.ds(k, 1)]).then_inc(e_fin.sem, 1)
                hold(pe, e_ot.sem, e_ot.at(it, h + 1))
                for q in range(SUP // 2):
                    i = h * (SUP // 2) + q
                    hold(pe, e_pr.sem, e_pr.at(it, i + 1 - 4))
                    for j in (2 * q, 2 * q + 1):
                        for p in range(3):
                            ins = pe.matmul(psw[q][:, (j % 2) * 256:(j % 2 + 1) * 256], oht[h][:, j * P:(j + 1) * P],
                                            table[:, p, :], start=(p == 0), stop=(p == 2))
                    ins.then_inc(e_w.sem, 1)
                hold(pe, e_fin.sem, e_fin.at(it, h + 1))
                hold(pe, e_ow.sem, e_ow.at(it, h + 1))
                hold(pe, e_su.sem, e_su.at(it, h - 1))
                for j in range(SUP):
                    ins = pe.matmul(psa[h][:, 0:C], ohw[h][:, j, :], msg[h][:, j, :], start=(j == 0), stop=(j == SUP - 1))
                ins.then_inc(e_acc.sem, 1)
                act.wait_ge(e_add[h].sem, e_add[h].at(it, 1))
                act.wait_ge(e_acc.sem, e_acc.at(it, h + 1))
                act.activation(sums[h][:, :], psa[h][:, 0:C], ACT.Copy).then_inc(e_su.sem, 1)
        su, fin = e_su.close(ITS), e_fin.close(ITS)
        added = [x.close(ITS) for x in e_add]
        need(pool, su, fin)
        for h in range(2):
            need(pool, added[1 - h])
            pool.indirect_dma_start(m_dram, bass.IndirectOffsetOnAxis(ap=ridx[h][:, 0:1], axis=0),
                                    sums[h][:, :], None, compute_op=ALU.add).then_inc(e_add[h].sem, 16)
            added[h] = (added[h][0], added[h][1] + 16)
        need(sp, *added)
        s.close()

    def split_matrix(stack, name, R, src, toks):
        T = sb(stack, name, [R, 3, 256], BF16)
        r = sb(stack, name + "_r", [R, 256])
        need(dve, *toks)
        link(dve, dve.tensor_copy(T[:, 0, :], src))
        link(dve, dve.tensor_tensor(r[:, :], src, T[:, 0, :], ALU.subtract))
        link(dve, dve.tensor_copy(T[:, 1, :], r[:, :]))
        return T, link(dve, dve.tensor_tensor(T[:, 2, :], r[:, :], T[:, 1, :], ALU.subtract))

    def store_h(tok):
        need(sp, tok)
        tok = s_load.by(sp.dma_start(h_dram.rearrange("(t p) f -> p t f", p=P), H[:, :, :]), 16)
        need(sp, tok)
        need(pool, tok)

    h_tok = norm(x_tok)
    store_h(h_tok)
    l1 = ExitStack()
    emb, tok = split_matrix(l1, "emb", R8, w("emb"), [])
    need(pe, tok)
    edge_layer("L1", R8, F, t["type_8"], emb, m1_dram)
    nc.all_engine_barrier()
    l1.close()
    gru = ExitStack()
    Z = sb(gru, "gru_in", [P, NT, 2 * F + 2])
    gates = sb(gru, "gates", [P, NT, 4 * F])
    d = dict(Y=sb(gru, "gru_Y", [2 * F + 2, NP]), ps=banks(gru, "gru_ps", 8), free={})
    m_tok = s_load.by(sp.dma_start(q1[:, :, :], m1_dram[0:NP, :].rearrange("(t p) f -> p t f", p=P)), 16)
    step(dve, dve.memset(Z[:, :, 2 * F:2 * F + 2], 1.0))
    step(dve, dve.tensor_copy(Z[:, :, F:2 * F], H[:, :, :]))
    need(dve, m_tok)
    z_tok = link(dve, dve.tensor_copy(Z[:, :, 0:F], q1[:, :, :]))
    y = to_features(d, Z, 2 * F + 2, [z_tok])
    need(pe, y[-1], *d["free"].values())
    for gr in range(NT // TG):
        bank = d["ps"][gr]
        for i in range(TG):
            n = (gr * TG + i) * P
            ins = pe.matmul(bank[:, i * 64:(i + 1) * 64], d["Y"][0:2 * F + 2, n:n + P], w("gru"), start=True, stop=True)
        need(act, step(pe, ins))
        src = bank[:, 0:TG * 64].rearrange("p (t f) -> p t f", f=64)
        g_tok = step(act, act.activation(gates[:, gr * TG:(gr + 1) * TG, :], src, ACT.Copy))
    need(act, g_tok)
    need(dve, step(act, act.activation(gates[:, :, 0:2 * F], gates[:, :, 0:2 * F], ACT.Sigmoid)))
    r_, z_, in_, hn_ = (gates[:, :, i * F:(i + 1) * F] for i in range(4))
    link(dve, dve.tensor_tensor(hn_, hn_, r_, ALU.mult))
    need(act, link(dve, dve.tensor_tensor(in_, in_, hn_, ALU.add)))
    need(dve, step(act, act.activation(in_, in_, ACT.Tanh)))
    link(dve, dve.tensor_tensor(hn_, H[:, :, :], in_, ALU.subtract))
    link(dve, dve.tensor_tensor(hn_, hn_, z_, ALU.mult))
    link(dve, dve.tensor_tensor(hn_, hn_, in_, ALU.add))
    x_tok = link(dve, dve.tensor_tensor(X[:, :, :], X[:, :, :], hn_, ALU.add))
    nc.all_engine_barrier()
    gru.close()

    h_tok = norm(x_tok)
    d = dense_scope("L2")
    y = to_features(d, H, F, [h_tok])
    rows, y = aggregate(d, F, table_from_Y(d, "gcn", F, F, [y[-1]]))
    y = feature_layer(d, "fold16", rows, F, y, "gcn_b", leaky=False)
    x_tok = to_nodes(d, [y[-1]])
    nc.all_engine_barrier()
    d["stack"].close()

    h_tok = norm(x_tok)
    store_h(h_tok)
    l3 = ExitStack()
    relT = sb(l3, "relT", [R90, 256])
    relO = sb(l3, "relO", [R90, 256])
    t_u = sb(l3, "t_u", [P, 3 * F])
    pre = ExitStack()
    pp = banks(pre, "rel_ps", 2)
    ptok = step(pe, pe.matmul(pp[0][0:R90, 0:256], w("w_comp"), w("V"), start=True, stop=True))
    for i in range(3):
        ins = pe.matmul(pp[1][:, i * F:(i + 1) * F], w(f"wa{i}"), w("ws"), start=True, stop=True)
    utok = step(pe, ins)
    need(dve, ptok)
    need(sp, step(dve, dve.tensor_copy(relT[:, :], pp[0][0:R90, 0:256])))
    need(dve, utok)
    step(dve, dve.tensor_copy(t_u[:, :], pp[1][:, 0:3 * F]))
    need(sp, s_load.by(sp.dma_start(rel_dram.rearrange("a r c -> r a c"), relT[:, :].rearrange("r (a c) -> r a c", a=F)), 16))
    need(dve, s_load.by(sp.dma_start(relT[:, :], rel_dram.rearrange("a r c -> (a r c)").rearrange("(r k) -> r k", k=256)), 16))
    tok = link(dve, dve.tensor_copy(relO[:, :].rearrange("r (o i) -> r o i", i=F), relT[:, :].rearrange("r (i o) -> r o i", o=F)))
    rel, tok = split_matrix(l3, "rel", R90, relO[:, :], [tok])
    need(pe, tok)
    nc.all_engine_barrier()
    pre.close()
    edge_layer("L3", R90, 2 * F, t["type_90"], rel, m3_dram, attr=t["he"])
    nc.all_engine_barrier()
    M = sb(l3, "M", [P, NT, 2 * F])
    m_tok = s_load.by(sp.dma_start(M[:, :, :], m3_dram[0:NP, :].rearrange("(t p) f -> p t f", p=P)), 16)
    link(dve, dve.tensor_tensor(q1[:, :, :], H[:, :, :], under(t_u[:, 2 * F:3 * F], NT), ALU.mult))
    link(dve, dve.tensor_reduce(mean[:, :], q1[:, :, :], AX.X, ALU.add))
    need(dve, m_tok)
    link(dve, dve.tensor_tensor(q1[:, :, :], M[:, :, F:2 * F], over(mean[:, :], F), ALU.mult))
    link(dve, dve.tensor_tensor(q1[:, :, :], q1[:, :, :], M[:, :, 0:F], ALU.add))
    x_tok = link(dve, dve.tensor_tensor(X[:, :, :], X[:, :, :], q1[:, :, :], ALU.add))
    need(sp, x_tok)
    full = (N // P) * P
    stored = s_load.by(sp.dma_start(out[0:full, :].rearrange("(t p) f -> p t f", p=P), X[:, 0:N // P, :]), 16)
    stored = s_load.by(sp.dma_start(out[full:N, :], X[0:N - full, N // P, :]), 16)
    need(sp, stored)
    l3.close()
    life.close()


def layout(inputs):
    import numpy as np

    a = {k: np.asarray(v) for k, v in inputs.items()}
    pad = EP - E
    x = np.zeros((NP, F), np.float32)
    x[:N] = a["x"]
    src = np.concatenate([a["src"].astype(np.int32), np.arange(pad, dtype=np.int32)])
    dst = np.concatenate([a["dst"].astype(np.int32), N + (np.arange(pad, dtype=np.int32) * (NP - N)) // pad])
    tiles = lambda v: np.ascontiguousarray(v.reshape(ET, P).T)
    none = np.full(P, -1, np.int32)
    zeros = np.zeros(pad, np.int32)
    he = np.zeros((EP, F), np.float32)
    he[:E] = a["edge_attr_16"]
    d = {
        "x": x, "src_pm": tiles(src), "dst_pm": tiles(dst), "dst_base": dst[::SE][None],
        "src_row": np.concatenate([none, src, none])[None], "dst_row": np.concatenate([none, dst, none])[None],
        "type_8": np.concatenate([a["edge_type_8"], zeros])[None], "type_90": np.concatenate([a["edge_type_90"], zeros])[None],
        "he": he.reshape(SG, SUP, P, F).transpose(0, 2, 1, 3).reshape(SG, P, SUP * F),
    }
    eye = np.eye(64, dtype=np.float32)
    g = lambda k: a["L0_gnn_" + k]
    ih, hh, bi, bh = (a["L1_gnn_" + k] for k in ("w_ih", "w_hh", "b_ih", "b_hh"))
    gru = np.zeros((2 * F + 2, 4 * F), np.float32)
    gru[0:F, 0:3 * F] = ih.T
    gru[F:2 * F, 0:2 * F] = hh[0:2 * F].T
    gru[F:2 * F, 3 * F:] = hh[2 * F:].T
    gru[2 * F, 0:3 * F] = bi
    gru[2 * F + 1, 0:2 * F] = bh[0:2 * F]
    gru[2 * F + 1, 3 * F:] = bh[2 * F:]
    ws = {
        "enc0": np.concatenate([g("enc_W0")] * 3), "enc1": np.concatenate([g("enc_W1")] * 2), "enc2": g("enc_W2"),
        "dec0": np.concatenate([g("dec_W0")] * 2), "dec1": g("dec_W1"), "dec2": g("dec_W2"),
        "lat0": g("lat_W0"), "lat1": g("lat_W1"), "dfc0": g("dfc_W0"), "dfc1": g("dfc_W1"),
        "eye64": eye, "fold64": np.concatenate([eye] * 2), "fold16": np.concatenate([eye[0:F, 0:F]] * 3),
        "gcn": a["L2_gnn_W"], "gcn_b": a["L2_gnn_b"][:, None], "gru": gru, "emb": a["L1_gnn_edge_emb"],
        "w_comp": a["L3_gnn_w_comp"].T, "V": a["L3_gnn_weight"].reshape(F, 30, F).transpose(1, 0, 2).reshape(30, F * F),
        "ws": a["L3_gnn_Ws"],
    }
    for i in range(3):
        ws[f"wa{i}"] = np.repeat(a["L3_gnn_Wa"][0, i * F:(i + 1) * F][:, None], P, 1)
    for k in ("enc_b0", "enc_b1", "enc_b2", "lat_b0", "lat_b1", "dfc_b0", "dfc_b1", "dec_b0", "dec_b1", "dec_b2"):
        ws[k] = g(k)[:, None]
    cols, at = {}, 0
    pack = np.zeros((P, sum(v.shape[1] for v in ws.values())), np.float32)
    for k, v in ws.items():
        cols[k] = (v.shape[0], at, at + v.shape[1])
        pack[:v.shape[0], at:at + v.shape[1]] = v
        at += v.shape[1]
    d["wpack"] = pack
    return {k: np.ascontiguousarray(v) for k, v in d.items()}, cols


def kernel(**inputs):
    import concourse.bacc as bacc
    from concourse.bass_utils import run_bass_kernel_spmd

    nc = bacc.Bacc("TRN2", target_bir_lowering=False, num_devices=1)
    arrays, cols = layout(inputs)
    t = {k: nc.dram_tensor(f"in_{k}", v.shape, mybir.dt.from_np(v.dtype), kind="ExternalInput").ap() for k, v in arrays.items()}
    out = nc.dram_tensor("out_x", (N, F), F32, kind="ExternalOutput").ap()
    program(nc, t, cols, out)
    r = run_bass_kernel_spmd(nc, [{f"in_{k}": v for k, v in arrays.items()}], core_ids=[0])
    return r.results[0]["out_x"]
```

```python
import concourse.bass as bass
from concourse import mybir
from contextlib import ExitStack

F32, BF16, F16, I32, U32 = mybir.dt.float32, mybir.dt.bfloat16, mybir.dt.float16, mybir.dt.int32, mybir.dt.uint32
FP8, U8 = mybir.dt.float8e4, mybir.dt.uint8
ALU = mybir.AluOpType
ACT = mybir.ActivationFunctionType
AX = mybir.AxisListType

P = 128
N, E, F = 6250, 206250, 16
NT = -(-N // P)
NP = NT * P
SUP = 8
BODY = 2 * SUP
ITS = -(-E // (P * BODY))
ET = ITS * BODY
EP = ET * P
SG = ET // SUP
SE = SUP * P
MROWS = NP + 2 * 64
SHIFT = 13
ROW = 1 << SHIFT
R8, R90 = 8, 90
MANY = 1024
BITS = 16
CH = 448
HALF = 7
RING = 7
TG = 7
EPS = 1e-5
SLOPE = 0.01
WIN = 64
ONE_FP8 = 0x38
TOP = 14
TINY = 2.0 ** -100



class Counted:

    def __init__(self, nc, name):
        self.sem = nc.alloc_semaphore(name)
        self.n = 0

    def by(self, ins, k=1):
        ins.then_inc(self.sem, k)
        self.n += k
        return (self.sem, self.n)


class Looped:

    def __init__(self, nc, name, per=1, step=1):
        self.sem, self.per, self.step, self.n0 = nc.alloc_semaphore(name), per, step, 0

    def credit(self, eng, depth):
        eng.sem_inc(self.sem, depth * self.step)
        self.n0 += depth * self.step

    def credit_dma(self, ins):
        ins.then_inc(self.sem, self.step)
        self.n0 += self.step

    def at(self, it, k):
        return it * (self.per * self.step) + (self.n0 + k * self.step)

    def close(self, its):
        self.n0 += its * self.per * self.step
        return (self.sem, self.n0)


def need(eng, *tokens):
    for sem, value in tokens:
        eng.wait_ge(sem, value)


def program(nc, t, wcols, out):
    pe, dve, act, pool, sp = nc.tensor, nc.vector, nc.scalar, nc.gpsimd, nc.sync
    engines = [pe.engine, dve.engine, act.engine, pool.engine, sp.engine]
    life = ExitStack()

    turns = nc.alloc_semaphore("turns")

    def hold(eng, sem, value):
        eng.wait_ge(sem, value)
        eng.sem_inc(turns, 1)

    done = {e: Counted(nc, f"done_{n}") for e, n in ((pe, "pe"), (dve, "dve"), (act, "act"), (pool, "pool"))}
    s_load = Counted(nc, "loaded")

    def step(eng, ins):
        return done[eng].by(ins)

    def link(eng, ins):
        tok = step(eng, ins)
        need(eng, tok)
        return tok

    def sb(stack, name, shape, dt=F32):
        return stack.enter_context(nc.sbuf_tensor(name, list(shape), dt))

    def banks(stack, name, n):
        return [stack.enter_context(nc.psum_tensor(f"{name}{b}", [P, 512], F32)) for b in range(n)]

    adj = nc.dram_tensor("adj", (NP * ROW, 1), U8).ap()
    adj_rows = adj.rearrange("(r c) o -> r (c o)", c=ROW)
    h_dram = nc.dram_tensor("h_rows", (NP, F), F32).ap()
    m1_dram = nc.dram_tensor("m1_rows", (2, MROWS, F), F32).ap()
    m3_dram = nc.dram_tensor("m3_rows", (2, MROWS, 2 * F), F32).ap()
    dinv_dram = nc.dram_tensor("dinv_row", (NT, P), F32).ap()
    rel_dram = nc.dram_tensor("rel_flat", (F, R90, F), F32).ap()

    X = sb(life, "X", [P, NT, F])
    W = sb(life, "W", [P, t["wpack"].shape[1]])
    I128 = sb(life, "I128", [P, P])
    dloc = sb(life, "dloc", [P, ET])
    baseI = sb(life, "baseI", [P, SG], I32)
    dinvN = sb(life, "dinvN", [P, NT])
    iotaP = sb(life, "iotaP", [P, 1])
    iotaPi = sb(life, "iotaPi", [P, 1], I32)
    iota128 = sb(life, "iota128", [P, P])
    bitno = sb(life, "bitno", [2 * BITS, 1], I32)
    H = sb(life, "H", [P, NT, F])
    q1 = sb(life, "q1", [P, NT, F])
    mean = sb(life, "mean", [P, NT])
    var = sb(life, "var", [P, NT])

    def w(name):
        r, c0, c1 = wcols[name]
        return W[0:r, c0:c1]

    def over(ap, n):
        return ap.rearrange("p (a o) -> p a o", o=1).to_broadcast([ap.shape[0], ap.shape[1], n])

    def under(ap, n):
        return ap.rearrange("p (o a) -> p o a", o=1).to_broadcast([ap.shape[0], n, ap.shape[1]])

    def norm(x_tok):
        need(dve, x_tok)
        link(dve, dve.tensor_reduce(mean[:, :], X[:, :, :], AX.X, ALU.add))
        link(dve, dve.tensor_scalar(mean[:, :], mean[:, :], 1.0 / F, None, ALU.mult))
        link(dve, dve.tensor_tensor(H[:, :, :], X[:, :, :], over(mean[:, :], F), ALU.subtract))
        link(dve, dve.tensor_tensor(q1[:, :, :], H[:, :, :], H[:, :, :], ALU.mult))
        link(dve, dve.tensor_reduce(var[:, :], q1[:, :, :], AX.X, ALU.add))
        need(act, link(dve, dve.tensor_scalar(var[:, :], var[:, :], 1.0 / F, EPS, ALU.mult, ALU.add)))
        need(dve, step(act, act.activation(var[:, :], var[:, :], ACT.Sqrt)))
        link(dve, dve.reciprocal(var[:, :], var[:, :]))
        link(dve, dve.tensor_tensor(H[:, :, :], H[:, :, :], over(var[:, :], F), ALU.mult))
        return link(dve, dve.tensor_scalar(H[:, :, :], H[:, :, :], 0.0, None, ALU.max))

    setup = ExitStack()
    dstI = sb(setup, "dstI", [P, ET], I32)
    srcI = sb(setup, "srcI", [P, ET], I32)
    iotaH = sb(setup, "iotaH", [P, P], I32)
    zrow = sb(setup, "zrow", [P, NP], U8)
    zf = sb(setup, "zf", [P, 2 * MROWS * F // P])
    zb = sb(setup, "zb", [P, P], BF16)
    ones = sb(setup, "ones", [P, NT], U8)
    need(sp, link(dve, dve.memset(zrow[:, :], 0)))
    step(dve, dve.memset(zb[:, :], 0.0))
    step(dve, dve.memset(zf[:, :], 0.0))
    need(sp, link(dve, dve.memset(ones[:, :], ONE_FP8)))

    def load(dst, src):
        return s_load.by(sp.dma_start(dst, src), 16)

    load(dstI[:, :], t["dst_pm"])
    load(srcI[:, :], t["src_pm"])
    load(baseI[:, :], t["dst_base"].to_broadcast([P, SG]))
    load(X[:, :, :], t["x"].rearrange("(t p) f -> p t f", p=P))
    loaded = load(W[:, :], t["wpack"])
    step(pool, pool.iota(iotaPi[:, :], pattern=[[0, 1]], base=0, channel_multiplier=1))
    step(pool, pool.iota(iota128[:, :], pattern=[[1, P]], base=0, channel_multiplier=0, allow_small_or_imprecise_dtypes=True))
    step(pool, pool.iota(iotaH[:, :], pattern=[[1, P]], base=0, channel_multiplier=0))
    link(pool, pool.memset(I128[:, :], 0.0))
    ready = step(pool, pool.affine_select(out=I128[:, :], in_=I128[:, :], compare_op=ALU.not_equal, fill=1.0,
                                          base=0, pattern=[[-1, P]], channel_multiplier=1))
    s_zero = Counted(nc, "zeroed")
    for k in range(NT):
        zeroed = s_zero.by(sp.dma_start(adj_rows[k * P:(k + 1) * P, 0:NP], zrow[:, :]), 16)
    s_sums = Counted(nc, "sums_zeroed")
    for m in (m1_dram, m3_dram[0:1], m3_dram[1:2]):
        s_sums.by(sp.dma_start(m.rearrange("s n c -> (s n c)").rearrange("(p k) -> p k", p=P), zf[:, :]), 16)
    need(sp, zeroed)
    s_diag = Counted(nc, "diagonal_set")
    with nc.allow_non_contiguous_dma(reason="the diagonal's cells"):
        for k in range(NT):
            cells = bass.AP(tensor=adj.tensor, offset=k * P * (ROW + 1), ap=[[ROW + 1, P], [1, 1]])
            diagonal = s_diag.by(sp.dma_start(cells, ones[:, k:k + 1]), 16)

    need(dve, loaded, ready)
    step(dve, dve.tensor_copy(iotaP[:, :], iotaPi[:, :]))
    step(dve, dve.tensor_scalar(bitno[:, :], iotaPi[0:2 * BITS, :], BITS - 1, None, ALU.bitwise_and))
    step(dve, dve.tensor_tensor(dloc[:, :].rearrange("p (s e) -> p s e", e=SUP),
                                dstI[:, :].rearrange("p (s e) -> p s e", e=SUP), over(baseI[:, :], SUP), ALU.subtract))
    h_tok = norm(loaded)

    build = ExitStack()
    SPAN = SE + 2 * P
    keyrow = [sb(build, f"keyrow{h}", [2 * BITS, SPAN], I32) for h in range(2)]
    keybit = [sb(build, f"keybit{h}", [2 * BITS, SPAN], I32) for h in range(2)]
    keypm = [sb(build, f"keypm{h}", [2 * BITS, SPAN], BF16) for h in range(2)]
    hit = sb(build, "hit", [P, 4, 3 * P], BF16)
    cnt = [sb(build, f"cnt{h}", [P, SUP]) for h in range(2)]
    same = [sb(build, f"same{h}", [P, SUP]) for h in range(2)]
    val = [sb(build, f"val{h}", [P, SUP], FP8) for h in range(2)]
    cell = [sb(build, f"cell{h}", [P, SUP], U32) for h in range(2)]
    later = [sb(build, f"later{h}", [P, SUP], I32) for h in range(2)]
    away = [sb(build, f"away{h}", [P, SUP], I32) for h in range(2)]
    spare = sb(build, "spare", [P, ET], I32)
    rank = sb(build, "rank", [P, 3 * P])
    dlo = sb(build, "dlo", [P, ET], I32)
    dhi = sb(build, "dhi", [P, ET], I32)
    ohlo = [sb(build, f"ohlo{h}", [P, SUP, P], BF16) for h in range(2)]
    ohhi = [sb(build, f"ohhi{h}", [P, SUP, NT], BF16) for h in range(2)]
    NDOT = 4
    dot = banks(build, "dot", NDOT)
    hist = build.enter_context(nc.psum_tensor("hist", [P, 512], F32))
    assert NP + ET <= ROW and MANY > 3 * P
    step(pool, pool.iota(spare[:, :], pattern=[[1, ET]], base=NP, channel_multiplier=ROW))
    step(pool, pool.memset(rank[:, 0:P], float(MANY)))
    link(pool, pool.memset(rank[:, P:2 * P], float(MANY + 1)))
    step(pool, pool.memset(rank[:, 2 * P:3 * P], 1.0))
    need(dve, step(pool, pool.affine_select(out=rank[:, P:2 * P], in_=rank[:, P:2 * P], compare_op=ALU.is_gt, fill=1.0,
                                            base=0, pattern=[[-1, P]], channel_multiplier=1)))
    step(dve, dve.tensor_scalar(dlo[:, :], dstI[:, :], P - 1, None, ALU.bitwise_and))
    cols = link(dve, dve.tensor_scalar(dhi[:, :], dstI[:, :], 7, None, ALU.logical_shift_right))

    b_row = [Looped(nc, f"b_row{h}", 2, 16) for h in range(2)]
    b_bit = Looped(nc, "b_bit", 2)
    b_pm = Looped(nc, "b_pm", 2)
    b_oh = Looped(nc, "b_oh", 2)
    b_dot = Looped(nc, "b_dot", BODY)
    b_mm = Looped(nc, "b_mm", 2)
    b_cnt = Looped(nc, "b_cnt", BODY)
    b_key = Looped(nc, "b_key", 2 * 7)
    b_val = Looped(nc, "b_val", 2)
    b_sc = [Looped(nc, f"b_sc{h}", SUP, 16) for h in range(2)]
    b_bit.credit(dve, 2)
    b_pm.credit(act, 2)
    b_mm.credit(pe, 2)
    b_cnt.credit(dve, NDOT)
    for h in range(2):
        b_sc[h].credit_dma(pool.dma_start(cell[h][:, :], t["src_pm"][:, 0:SUP].bitcast(U32)))
    need(pe, cols)
    step(pe, pe.matmul(hist[:, 0:NT], zb[:, 0:P], zb[:, 0:NT], start=True, stop=False, skip_group_check=True))
    need(pool, diagonal)
    need(dve, cols)
    with nc.Fori(0, ITS, engines=engines) as it:
        for h in range(2):
            k = 2 * it + h
            sp.wait_ge(b_bit.sem, b_bit.at(it, h - 1))
            win = bass.ds(k * SE, SPAN)
            sp.dma_start(keyrow[h][0:BITS, :], t["src_row"][:, win].to_broadcast([BITS, SPAN])).then_inc(b_row[h].sem, 16)
            sp.dma_start(keyrow[h][BITS:2 * BITS, :], t["dst_row"][:, win].to_broadcast([BITS, SPAN])).then_inc(b_row[h].sem, 16)
            dve.wait_ge(b_pm.sem, b_pm.at(it, h - 1))
            dve.wait_ge(b_row[h].sem, b_row[h].at(it, 2))
            dve.tensor_scalar(keybit[h][:, :], keyrow[h][:, :], bitno[:, 0:1], 1,
                              ALU.logical_shift_right, ALU.bitwise_and).then_inc(b_bit.sem, 1)
            act.wait_ge(b_mm.sem, b_mm.at(it, h - 1))
            act.wait_ge(b_bit.sem, b_bit.at(it, h + 1))
            act.activation(keypm[h][:, :], keybit[h][:, :], ACT.Copy, bias=-1.0, scale=2.0).then_inc(b_pm.sem, 1)
            dve.wait_ge(b_mm.sem, b_mm.at(it, h - 1))
            e8 = bass.ds(k * SUP, SUP)
            dve.tensor_tensor(ohlo[h][:, :, :], under(iotaH[:, :], SUP), over(dlo[:, e8], P), ALU.is_equal)
            dve.tensor_tensor(ohhi[h][:, :, :], under(iotaH[:, 0:NT], SUP), over(dhi[:, e8], NT),
                              ALU.is_equal).then_inc(b_oh.sem, 1)
            hold(pe, b_pm.sem, b_pm.at(it, h + 1))
            for j in range(SUP):
                i = h * SUP + j
                hold(pe, b_cnt.sem, b_cnt.at(it, i + 1 - NDOT))
                pe.matmul(dot[j % NDOT][:, 0:3 * P], keypm[h][:, (j + 1) * P:(j + 2) * P], keypm[h][:, j * P:(j + 3) * P],
                          start=True, stop=True).then_inc(b_dot.sem, 1)
            hold(pe, b_oh.sem, b_oh.at(it, h + 1))
            for j in range(SUP):
                ins = pe.matmul(hist[:, 0:NT], ohlo[h][:, j, :], ohhi[h][:, j, :], start=False, stop=False,
                                skip_group_check=True)
            ins.then_inc(b_mm.sem, 1)
            dve.wait_ge(b_sc[h].sem, b_sc[h].at(it, 0))
            for j in range(SUP):
                i = h * SUP + j
                dve.wait_ge(b_dot.sem, b_dot.at(it, i + 1))
                dve.scalar_tensor_tensor(hit[:, j % 4, :], dot[j % NDOT][:, 0:3 * P], float(2 * BITS), rank[:, :],
                                         ALU.is_equal, ALU.mult, accum_out=cnt[h][:, j:j + 1]).then_inc(b_cnt.sem, 1)
            dve.tensor_tensor(same[h][:, :], srcI[:, e8], dstI[:, e8], ALU.is_equal).then_inc(b_key.sem, 1)
            dve.tensor_scalar(cell[h][:, :].bitcast(I32), srcI[:, e8], SHIFT, None, ALU.logical_shift_left).then_inc(b_key.sem, 1)
            dve.wait_ge(b_cnt.sem, b_cnt.at(it, (h + 1) * SUP))
            c8 = cell[h][:, :].bitcast(I32)
            hold(dve, b_key.sem, b_key.at(it, 7 * h + 2))
            dve.tensor_tensor(val[h][:, :], cnt[h][:, :], same[h][:, :], ALU.add, saturate=False).then_inc(b_key.sem, 1)
            dve.tensor_tensor(c8, c8, dstI[:, e8], ALU.bitwise_or).then_inc(b_key.sem, 1)
            dve.tensor_scalar(later[h][:, :], cnt[h][:, :], float(MANY), -1.0, ALU.is_ge, ALU.mult).then_inc(b_key.sem, 1)
            dve.wait_ge(b_key.sem, b_key.at(it, 7 * h + 5))
            dve.tensor_tensor(away[h][:, :], later[h][:, :], spare[:, e8], ALU.bitwise_and).then_inc(b_key.sem, 1)
            dve.scalar_tensor_tensor(c8, later[h][:, :], -1, c8, ALU.bitwise_xor, ALU.bitwise_and).then_inc(b_key.sem, 1)
            dve.wait_ge(b_key.sem, b_key.at(it, 7 * h + 7))
            dve.tensor_tensor(c8, c8, away[h][:, :], ALU.bitwise_or).then_inc(b_val.sem, 1)
            hold(pool, b_val.sem, b_val.at(it, h + 1))
            for j in range(SUP):
                pool.indirect_dma_start(adj, bass.IndirectOffsetOnAxis(ap=cell[h][:, j:j + 1], axis=0),
                                        val[h][:, j:j + 1].bitcast(U8), None).then_inc(b_sc[h].sem, 16)
    scattered = [s.close(ITS) for s in b_sc]
    counted = b_mm.close(ITS)
    need(dve, counted)
    link(dve, dve.tensor_scalar(dinvN[:, :], hist[:, 0:NT], 1.0, None, ALU.add))
    need(act, (done[dve].sem, done[dve].n))
    need(dve, step(act, act.activation(dinvN[:, :], dinvN[:, :], ACT.Sqrt)))
    need(pe, link(dve, dve.reciprocal(dinvN[:, :], dinvN[:, :])))
    need(dve, step(pe, pe.transpose(dot[0][0:NT, 0:P], dinvN[:, :], I128[:, :])))
    dinvT = sb(build, "dinvT", [NT, P])
    need(sp, step(dve, dve.tensor_copy(dinvT[:, :], dot[0][0:NT, 0:P])))
    need(sp, s_load.by(sp.dma_start(dinv_dram, dinvT[:, :]), 16))
    need(sp, *scattered)
    need(sp, (s_sums.sem, s_sums.n))
    nc.all_engine_barrier()
    build.close()
    setup.close()

    def dense_scope(name):
        s = ExitStack()
        d = dict(
            ring=[sb(s, f"{name}_ring{j}", [P, HALF * CH], U8) for j in range(RING)],
            Y=sb(s, f"{name}_Y", [P, NP]),
            T=sb(s, f"{name}_T", [P, NT, 2 * 64], F16),
            peak=sb(s, f"{name}_peak", [P, NT // TG + 1]),
            top=sb(s, f"{name}_top", [1, 4]),
            scale=sb(s, f"{name}_scale", [P, 2]),
            onerow=sb(s, f"{name}_onerow", [1, P]),
            tmp=sb(s, f"{name}_tmp", [P, NT, 64]),
            dinvB=sb(s, f"{name}_dinvB", [P, NP]),
            ps=banks(s, f"{name}_ps", 8),
            stage=[sb(s, f"{name}_stage{j}", [P, 2 * 64], F16) for j in range(RING)],
            s_stage=Counted(nc, f"{name}_staged"),
            s_in=[Counted(nc, f"{name}_in{j}") for j in range(RING)],
            s_row=Counted(nc, f"{name}_row"),
            free={},
            stack=s)
        s_d = Counted(nc, f"{name}_dinv")
        step(dve, dve.memset(d["onerow"][:, :], 1.0))
        flat = dinv_dram.rearrange("(o t) p -> o (t p)", o=1)
        d["dinv_tok"] = s_d.by(act.dma_start(d["dinvB"][:, :], flat.to_broadcast([P, NP])), 16)
        return d

    def split_table(d, Fo, sources, free):
        T, tmp, peak, top, scale = d["T"], d["tmp"], d["peak"], d["top"], d["scale"]
        need(dve, *free)
        need(act, *free)
        groups = range(NT // TG)
        G = NT // TG

        def part(g, p):
            return T[:, g * TG:(g + 1) * TG, p * Fo:(p + 1) * Fo]

        def tm(g):
            return tmp[:, g * TG:(g + 1) * TG, 0:Fo]

        for g in groups:
            src, toks = sources(g)
            need(dve, *toks)
            link(dve, dve.tensor_tensor(tm(g), src, over(dinvN[:, g * TG:(g + 1) * TG], Fo), ALU.mult))
            link(dve, dve.tensor_reduce(peak[:, g:g + 1], tm(g), AX.XY, ALU.max, apply_absolute_value=True))
        need(pe, link(dve, dve.tensor_reduce(peak[:, G:G + 1], peak[:, 0:G], AX.X, ALU.max)))
        need(pe, *bank_free(d, 7))
        need(dve, step(pe, pe.transpose(d["ps"][7][0:1, 0:P], peak[:, G:G + 1], I128[:, :])))
        link(dve, dve.tensor_reduce(top[:, 0:1], d["ps"][7][0:1, 0:P], AX.X, ALU.max))
        link(dve, dve.tensor_scalar(top[:, 0:1], top[:, 0:1], TINY, None, ALU.max))
        link(dve, dve.tensor_scalar(top[:, 1:2].bitcast(I32), top[:, 0:1].bitcast(I32), 0x7F800000, None, ALU.bitwise_and))
        link(dve, dve.tensor_scalar(top[:, 2:3].bitcast(I32), top[:, 1:2].bitcast(I32), -1.0, float((254 + TOP) << 23), ALU.mult, ALU.add))
        need(pe, link(dve, dve.tensor_scalar(top[:, 3:4], top[:, 1:2], 2.0 ** -TOP, None, ALU.mult)))
        need(dve, step(pe, pe.matmul(d["ps"][7][:, 256:258], d["onerow"][:, :], top[:, 2:4], start=True, stop=True)))
        sc = link(dve, dve.tensor_copy(scale[:, :], d["ps"][7][:, 256:258]))
        d["free"][7] = sc
        need(act, sc)
        for g in groups:
            need(dve, step(act, act.activation(part(g, 0), tm(g), ACT.Copy, scale=scale[:, 0:1])))
            last = step(dve, dve.scalar_tensor_tensor(part(g, 1), tm(g), scale[:, 0:1], part(g, 0), ALU.mult, ALU.subtract))
        return last

    def aggregate(d, Fo, table_toks):
        rows = 2 * Fo
        T, ring, ps, s_in, s_row = d["T"], d["ring"], d["ps"], d["s_in"], d["s_row"]
        out = []
        need(pe, *table_toks, *d["free"].values())
        evac = []
        for half in range(2):
            col = half * HALF * CH

            def load_row(j, row_ap):
                return sp.dma_start(ring[j][:, :], row_ap)

            def products(table, j, first):
                for c in range(HALF):
                    if first and evac:
                        need(pe, evac[c])
                    a = ring[j][:, c * CH:(c + 1) * CH].bitcast(FP8)
                    ins = pe.matmul(ps[c][0:rows, 0:CH], table, a, start=first, stop=False, skip_group_check=True)
                return ins

            for j in range(RING):
                if s_row.n:
                    need(sp, (s_row.sem, s_row.n - RING + j + 1))
                s_in[j].by(load_row(j, adj_rows[j * P:(j + 1) * P, col:col + HALF * CH]), 16)
            in0 = [s.n for s in s_in]
            row0 = s_row.n
            for j in range(RING):
                need(pe, (s_in[j].sem, s_in[j].n))
                s_row.by(products(T[:, j, 0:rows], j, j == 0))
            stage, s_stage = d["stage"], d["s_stage"]
            with nc.Fori(1, NT // RING, engines=[pe.engine, sp.engine, act.engine]) as it:
                for j in range(RING):
                    sp.wait_ge(s_row.sem, it * RING + (row0 - RING + j + 1))
                    load_row(j, adj_rows[bass.ds(it * (RING * P) + j * P, P), col:col + HALF * CH]).then_inc(s_in[j].sem, 16)
                for j in range(RING):
                    act.wait_ge(s_row.sem, it * RING + (row0 - RING + j + 1))
                    act.activation(stage[j][:, 0:rows], T[:, bass.ds(it * RING + j, 1), 0:rows].rearrange("p o c -> p (o c)"),
                                   ACT.Copy).then_inc(s_stage.sem, 1)
                for j in range(RING):
                    hold(pe, s_in[j].sem, it * 16 + in0[j])
                    hold(pe, s_stage.sem, it * RING + (s_stage.n - RING + j + 1))
                    products(stage[j][:, 0:rows], j, False).then_inc(s_row.sem, 1)
            s_stage.n += RING * (NT // RING - 1)
            for j in range(RING):
                s_in[j].n += 16 * (NT // RING - 1)
            s_row.n += RING * (NT // RING - 1)
            need(dve, (s_row.sem, s_row.n), d["dinv_tok"])
            evac = []
            for c in range(HALF):
                cc = slice(col + c * CH, col + (c + 1) * CH)
                d["free"][c] = (done[dve].sem, done[dve].n + 1)
                evac.append(step(dve, dve.scalar_tensor_tensor(
                    d["Y"][0:rows, cc], ps[c][0:rows, 0:CH], d["scale"][0:rows, 1:2], d["dinvB"][0:rows, cc], ALU.mult, ALU.mult)))
            out += evac
        return rows, out

    def bank_free(d, b):
        return [d["free"][b]] if b in d["free"] else []

    def feature_layer(d, name, rows, Fo, toks, bias, leaky=True):
        Y, ps = d["Y"], d["ps"]
        outs = []
        for c in range(2 * HALF):
            cc = slice(c * CH, (c + 1) * CH)
            bank = ps[c % 8]
            need(pe, toks[c], *bank_free(d, c % 8))
            need(act, step(pe, pe.matmul(bank[0:Fo, 0:CH], w(name), Y[0:rows, cc], start=True, stop=True)))
            outs.append(step(act, act.activation(Y[0:Fo, cc], bank[0:Fo, 0:CH], ACT.Identity, bias=w(bias))))
            d["free"][c % 8] = outs[-1]
            if leaky:
                need(dve, outs[-1])
                outs[-1] = step(dve, dve.scalar_tensor_tensor(Y[0:Fo, cc], Y[0:Fo, cc], SLOPE, Y[0:Fo, cc], ALU.mult, ALU.max))
        return outs

    def table_from_Y(d, name, Fi, Fo, toks):
        ps = d["ps"]
        free = list(toks)
        tks = {}

        def sources(g):
            bank = ps[g]
            need(pe, *toks, *bank_free(d, g))
            d["free"][g] = (done[dve].sem, done[dve].n + 1)
            for i in range(TG):
                n = (g * TG + i) * P
                tok = pe.matmul(bank[:, i * Fo:(i + 1) * Fo], d["Y"][0:Fi, n:n + P], w(name), start=True, stop=True)
            tok = step(pe, tok)
            return bank[:, 0:TG * Fo].rearrange("p (t f) -> p t f", f=Fo), [tok]

        return [split_table(d, Fo, sources, free)]

    def to_nodes(d, toks, extra=None):
        ps = d["ps"]
        need(pe, *toks)
        per = 512 // F
        outs = []
        for b in range(0, NT, per):
            m = min(per, NT - b)
            bank = ps[b // per]
            need(pe, *bank_free(d, b // per))
            for i in range(m):
                n = (b + i) * P
                ins = pe.transpose(bank[:, i * F:(i + 1) * F], d["Y"][0:F, n:n + P], I128[0:F, 0:F])
            need(dve, step(pe, ins))
            src = bank[:, 0:m * F].rearrange("p (t f) -> p t f", f=F)
            outs.append(link(dve, dve.tensor_tensor(X[:, b:b + m, :], X[:, b:b + m, :], src, ALU.add)))
        return outs[-1]

    def to_features(d, src, Fi, toks):
        outs = []
        need(pe, *toks)
        for b in range(0, NT, 4):
            m = min(4, NT - b)
            bank = d["ps"][(b // 4) % 8]
            need(pe, *bank_free(d, (b // 4) % 8))
            for i in range(m):
                ins = pe.transpose(bank[0:Fi, i * P:(i + 1) * P], src[:, b + i, :], I128[:, :])
            need(dve, step(pe, ins))
            outs.append(step(dve, dve.tensor_copy(d["Y"][0:Fi, b * P:(b + m) * P], bank[0:Fi, 0:m * P])))
            d["free"][(b // 4) % 8] = outs[-1]
        return outs

    def chunkwise(toks):
        return [toks[-1]] * (2 * HALF)

    d = dense_scope("L0")
    tmp = d["tmp"]
    last = split_table(d, F, lambda g: (H[:, g * TG:(g + 1) * TG, :], []), [h_tok])
    rows, y = aggregate(d, F, [last])
    y = feature_layer(d, "enc0", rows, 64, y, "enc_b0")
    rows, y = aggregate(d, 64, table_from_Y(d, "eye64", 64, 64, y))
    y = feature_layer(d, "enc1", rows, 128, y, "enc_b1")
    rows, y = aggregate(d, 64, table_from_Y(d, "enc2", 128, 64, y))
    y = feature_layer(d, "fold64", rows, 64, y, "enc_b2")
    y = feature_layer(d, "lat0", 64, 32, y, "lat_b0")
    y = feature_layer(d, "lat1", 32, 3, y, "lat_b1", leaky=False)
    y = feature_layer(d, "dfc0", 3, 32, y, "dfc_b0")
    y = feature_layer(d, "dfc1", 32, 64, y, "dfc_b1")
    rows, y = aggregate(d, 64, table_from_Y(d, "eye64", 64, 64, y))
    y = feature_layer(d, "dec0", rows, 128, y, "dec_b0")
    rows, y = aggregate(d, 64, table_from_Y(d, "dec1", 128, 64, y))
    y = feature_layer(d, "fold64", rows, 64, y, "dec_b1")
    rows, y = aggregate(d, F, table_from_Y(d, "dec2", 64, F, y))
    y = feature_layer(d, "fold16", rows, F, y, "dec_b2")
    need(act, *y)
    for half in range(2):
        hs = slice(half * HALF * CH, (half + 1) * HALF * CH)
        y.append(step(act, act.activation(d["Y"][0:F, hs], d["Y"][0:F, hs], ACT.Tanh)))
    x_tok = to_nodes(d, y[-2:])
    nc.all_engine_barrier()
    d["stack"].close()

    def edge_layer(name, R, types, table, m_dram, attr=None, u=None):
        s = ExitStack()
        C = F if attr is None else 2 * F
        PAIRS = SUP // 2
        NM = PAIRS if attr is None else PAIRS + 1
        g = [sb(s, f"{name}_g{h}", [P, SUP, F]) for h in range(2)]
        gidx = [sb(s, f"{name}_gi{h}", [P, SUP], U32) for h in range(2)]
        trow = [sb(s, f"{name}_tr{h}", [R, SE], I32) for h in range(2)]
        oht = [sb(s, f"{name}_ot{h}", [R, SE], BF16) for h in range(2)]
        ohw = [sb(s, f"{name}_ow{h}", [P, SUP, WIN]) for h in range(2)]
        prod = [sb(s, f"{name}_pr{q}", [P, 2, F, F]) for q in range(PAIRS)]
        msg = [sb(s, f"{name}_ms{h}", [P, SUP, C]) for h in range(2)]
        sums = [sb(s, f"{name}_su{h}", [WIN, C]) for h in range(2)]
        psw = banks(s, f"{name}_w", PAIRS)
        psa = banks(s, f"{name}_a", 2)
        if attr is not None:
            he = [sb(s, f"{name}_he{h}", [P, SUP, F]) for h in range(2)]
            ea = [sb(s, f"{name}_ea{h}", [P, SUP, F]) for h in range(2)]
            eb = [sb(s, f"{name}_eb{h}", [P, SUP, F]) for h in range(2)]
            e_ = [sb(s, f"{name}_e{h}", [P, SUP]) for h in range(2)]
        L = lambda n, per=2, st=1: Looped(nc, f"{name}_{n}", per, st)
        nr = 1 if attr is None else 2
        e_idx = [L(f"idx{h}", 1, 16) for h in range(2)]
        e_row = [L(f"row{h}", nr, 16) for h in range(2)]
        e_g = [L(f"g{h}", SUP, 16) for h in range(2)]
        e_out = [L(f"out{h}", 1, 16) for h in range(2)]
        e_ot = L("ot")
        e_ow = L("ow")
        e_e = L("e", 8)
        e_w = L("w", 2 * PAIRS)
        e_pr = L("pr", 2 * PAIRS)
        e_msg = L("msg", 2 * NM)
        e_sum = L("sum")
        e_su = L("su")
        for x, eng, depth in ((e_ot, dve, 2), (e_pr, dve, 2 * PAIRS), (e_w, pe, 2 * PAIRS), (e_sum, pe, 2), (e_su, act, 2), (e_msg, dve, 2 * NM)):
            x.credit(eng, depth)
        for h in range(2):
            e_g[h].credit_dma(pool.dma_start(g[h][:, 0, :], h_dram[0:P, :]))
            e_out[h].credit_dma(act.dma_start(sums[h][:, 0:F], h_dram[0:WIN, :]))

        def matrices(it, h):
            hold(pe, e_ot.sem, e_ot.at(it, h + 1))
            for q in range(PAIRS):
                hold(pe, e_pr.sem, e_pr.at(it, h * PAIRS + q + 1 - PAIRS))
                for j in (2 * q, 2 * q + 1):
                    for p in range(3):
                        ins = pe.matmul(psw[q][:, (j % 2) * 256:(j % 2 + 1) * 256], oht[h][:, j * P:(j + 1) * P],
                                        table[:, p, :], start=(p == 0), stop=(p == 2))
                ins.then_inc(e_w.sem, 1)

        def type_onehots(it, h):
            dve.wait_ge(e_row[h].sem, e_row[h].at(it, nr))
            dve.wait_ge(e_w.sem, e_w.at(it, (h - 1) * PAIRS))
            dve.tensor_scalar(oht[h][:, :], trow[h][:, :], iotaP[0:R, :], None, ALU.is_equal).then_inc(e_ot.sem, 1)

        def message_sums(it, h):
            hold(pe, e_ow.sem, e_ow.at(it, h + 1))
            hold(pe, e_su.sem, e_su.at(it, h - 1))
            hold(pe, e_msg.sem, e_msg.at(it, (h + 1) * NM))
            for j in range(SUP):
                ins = pe.matmul(psa[h][0:WIN, 0:C], ohw[h][:, j, :], msg[h][:, j, :], start=(j == 0), stop=(j == SUP - 1))
            ins.then_inc(e_sum.sem, 1)

        def edges(it, more):
            for h in range(2):
                k = 2 * it + h
                sp.wait_ge(e_g[h].sem, e_g[h].at(it, 0))
                sp.dma_start(gidx[h][:, :], t["src_pm"][:, bass.ds(k * SUP, SUP)].bitcast(U32)).then_inc(e_idx[h].sem, 16)
                sp.wait_ge(e_ot.sem, e_ot.at(it, h - 1))
                sp.dma_start(trow[h][:, :], types[:, bass.ds(k * SE, SE)].to_broadcast([R, SE])).then_inc(e_row[h].sem, 16)
                if attr is not None:
                    sp.wait_ge(e_pr.sem, e_pr.at(it, (h - 1) * PAIRS - PAIRS + 1))
                    sp.dma_start(he[h][:, :, :].rearrange("p e f -> p (e f)"),
                                 attr[bass.ds(k, 1), :, :].rearrange("o p c -> p (o c)")).then_inc(e_row[h].sem, 16)
                hold(pool, e_idx[h].sem, e_idx[h].at(it, 1))
                for q in range(PAIRS):
                    hold(pool, e_pr.sem, e_pr.at(it, (h - 2) * PAIRS + q + 1))
                    for j in (2 * q, 2 * q + 1):
                        pool.indirect_dma_start(g[h][:, j, :], None, h_dram,
                                                bass.IndirectOffsetOnAxis(ap=gidx[h][:, j:j + 1], axis=0)).then_inc(e_g[h].sem, 16)
                dve.wait_ge(e_sum.sem, e_sum.at(it, h - 1))
                dve.tensor_tensor(ohw[h][:, :, :], under(iota128[:, 0:WIN], SUP), over(dloc[:, bass.ds(k * SUP, SUP)], WIN),
                                  ALU.is_equal).then_inc(e_ow.sem, 1)
                dve.wait_ge(e_g[h].sem, e_g[h].at(it, SUP))
                if attr is not None:
                    dve.tensor_tensor(ea[h][:, :, :], g[h][:, :, :], under(u[:, 0:F], SUP), ALU.mult).then_inc(e_e.sem, 1)
                    dve.tensor_tensor(eb[h][:, :, :], he[h][:, :, :], under(u[:, F:2 * F], SUP), ALU.mult).then_inc(e_e.sem, 1)

                def product(q):
                    dve.wait_ge(e_w.sem, e_w.at(it, h * PAIRS + q + 1))
                    dve.wait_ge(e_msg.sem, e_msg.at(it, (h - 1) * NM + q + 1))
                    wq = psw[q][:, :].rearrange("p (t o i) -> p t o i", t=2, o=F)
                    gq = g[h][:, 2 * q:2 * q + 2, :].rearrange("p t (z i) -> p t z i", z=1).to_broadcast([P, 2, F, F])
                    dve.tensor_tensor(prod[q][:, :, :, :], wq, gq, ALU.mult).then_inc(e_pr.sem, 1)

                def message(q):
                    dve.wait_ge(e_pr.sem, e_pr.at(it, h * PAIRS + q + 1))
                    dve.tensor_reduce(msg[h][:, 2 * q:2 * q + 2, 0:F], prod[q][:, :, :, :], AX.X, ALU.add).then_inc(e_msg.sem, 1)

                product(0)
                if attr is not None:
                    dve.wait_ge(e_e.sem, e_e.at(it, 4 * h + 2))
                    dve.tensor_tensor(ea[h][:, :, :], ea[h][:, :, :], eb[h][:, :, :], ALU.add).then_inc(e_e.sem, 1)
                product(1)
                message(0)
                product(2)
                if attr is not None:
                    dve.wait_ge(e_e.sem, e_e.at(it, 4 * h + 3))
                    dve.tensor_reduce(e_[h][:, :], ea[h][:, :, :], AX.X, ALU.add).then_inc(e_e.sem, 1)
                product(3)
                if h == 0:
                    type_onehots(it, 1)
                elif more:
                    type_onehots(it + 1, 0)
                for q in range(1, PAIRS):
                    message(q)
                if attr is not None:
                    dve.wait_ge(e_e.sem, e_e.at(it, 4 * h + 4))
                    dve.wait_ge(e_msg.sem, e_msg.at(it, h * NM + PAIRS))
                    dve.tensor_tensor(msg[h][:, :, F:C], msg[h][:, :, 0:F], over(e_[h][:, :], F), ALU.mult).then_inc(e_msg.sem, 1)
                if h == 0:
                    matrices(it, 1)
                elif more:
                    matrices(it + 1, 0)
                message_sums(it, h)
                base = act.value_load(baseI[0:1, bass.ds(k, 1)], min_val=0, max_val=MROWS - WIN)
                act.wait_ge(e_out[h].sem, e_out[h].at(it, 0))
                act.wait_ge(e_sum.sem, e_sum.at(it, h + 1))
                act.activation(sums[h][:, :], psa[h][0:WIN, 0:C], ACT.Copy).then_inc(e_su.sem, 1)
                act.wait_ge(e_su.sem, e_su.at(it, h + 1))
                act.dma_start(m_dram[h, bass.ds(base, WIN), :], sums[h][:, :]).then_inc(e_out[h].sem, 16)

        type_onehots(0, 0)
        matrices(0, 0)
        with nc.Fori(0, ITS - 1, engines=engines) as it:
            edges(it, True)
        edges(ITS - 1, False)
        landed = [x.close(ITS) for x in e_out]
        need(sp, *landed)
        s.close()

    def split_matrix(stack, name, R, src, toks):
        T = sb(stack, name, [R, 3, 256], BF16)
        r = sb(stack, name + "_r", [R, 256])
        need(dve, *toks)
        link(dve, dve.tensor_copy(T[:, 0, :], src))
        link(dve, dve.tensor_tensor(r[:, :], src, T[:, 0, :], ALU.subtract))
        link(dve, dve.tensor_copy(T[:, 1, :], r[:, :]))
        return T, link(dve, dve.tensor_tensor(T[:, 2, :], r[:, :], T[:, 1, :], ALU.subtract))

    def store_h(tok):
        need(sp, tok)
        tok = s_load.by(sp.dma_start(h_dram.rearrange("(t p) f -> p t f", p=P), H[:, :, :]), 16)
        need(sp, tok)
        need(pool, tok)
        need(act, tok)

    h_tok = norm(x_tok)
    store_h(h_tok)
    l1 = ExitStack()
    emb, tok = split_matrix(l1, "emb", R8, w("emb"), [])
    need(pe, tok)
    edge_layer("L1", R8, t["type_8"], emb, m1_dram)
    nc.all_engine_barrier()
    l1.close()
    gru = ExitStack()
    Z = sb(gru, "gru_in", [P, NT, 2 * F + 2])
    gates = sb(gru, "gates", [P, NT, 4 * F])
    d = dict(Y=sb(gru, "gru_Y", [2 * F + 2, NP]), ps=banks(gru, "gru_ps", 8), free={})
    m = [sb(gru, f"gru_m{i}", [P, NT, F]) for i in range(2)]
    for i in range(2):
        m_tok = s_load.by(sp.dma_start(m[i][:, :, :], m1_dram[i, 0:NP, :].rearrange("(t p) f -> p t f", p=P)), 16)
    step(dve, dve.memset(Z[:, :, 2 * F:2 * F + 2], 1.0))
    step(dve, dve.tensor_copy(Z[:, :, F:2 * F], H[:, :, :]))
    need(dve, m_tok)
    z_tok = link(dve, dve.tensor_tensor(Z[:, :, 0:F], m[0][:, :, :], m[1][:, :, :], ALU.add))
    y = to_features(d, Z, 2 * F + 2, [z_tok])
    need(pe, y[-1], *d["free"].values())
    for gr in range(NT // TG):
        bank = d["ps"][gr]
        for i in range(TG):
            n = (gr * TG + i) * P
            ins = pe.matmul(bank[:, i * 64:(i + 1) * 64], d["Y"][0:2 * F + 2, n:n + P], w("gru"), start=True, stop=True)
        need(act, step(pe, ins))
        src = bank[:, 0:TG * 64].rearrange("p (t f) -> p t f", f=64)
        g_tok = step(act, act.activation(gates[:, gr * TG:(gr + 1) * TG, :], src, ACT.Copy))
    need(act, g_tok)
    need(dve, step(act, act.activation(gates[:, :, 0:2 * F], gates[:, :, 0:2 * F], ACT.Sigmoid)))
    r_, z_, in_, hn_ = (gates[:, :, i * F:(i + 1) * F] for i in range(4))
    link(dve, dve.tensor_tensor(hn_, hn_, r_, ALU.mult))
    need(act, link(dve, dve.tensor_tensor(in_, in_, hn_, ALU.add)))
    need(dve, step(act, act.activation(in_, in_, ACT.Tanh)))
    link(dve, dve.tensor_tensor(hn_, H[:, :, :], in_, ALU.subtract))
    link(dve, dve.tensor_tensor(hn_, hn_, z_, ALU.mult))
    link(dve, dve.tensor_tensor(hn_, hn_, in_, ALU.add))
    x_tok = link(dve, dve.tensor_tensor(X[:, :, :], X[:, :, :], hn_, ALU.add))
    nc.all_engine_barrier()
    gru.close()

    h_tok = norm(x_tok)
    d = dense_scope("L2")
    y = to_features(d, H, F, [h_tok])
    rows, y = aggregate(d, F, table_from_Y(d, "gcn", F, F, [y[-1]]))
    y = feature_layer(d, "fold16", rows, F, y, "gcn_b", leaky=False)
    x_tok = to_nodes(d, [y[-1]])
    nc.all_engine_barrier()
    d["stack"].close()

    h_tok = norm(x_tok)
    store_h(h_tok)
    l3 = ExitStack()
    relT = sb(l3, "relT", [R90, 256])
    relO = sb(l3, "relO", [R90, 256])
    t_u = sb(l3, "t_u", [P, 3 * F])
    pre = ExitStack()
    pp = banks(pre, "rel_ps", 2)
    ptok = step(pe, pe.matmul(pp[0][0:R90, 0:256], w("w_comp"), w("V"), start=True, stop=True))
    for i in range(3):
        ins = pe.matmul(pp[1][:, i * F:(i + 1) * F], w(f"wa{i}"), w("ws"), start=True, stop=True)
    utok = step(pe, ins)
    need(dve, ptok)
    need(sp, step(dve, dve.tensor_copy(relT[:, :], pp[0][0:R90, 0:256])))
    need(dve, utok)
    step(dve, dve.tensor_copy(t_u[:, :], pp[1][:, 0:3 * F]))
    need(sp, s_load.by(sp.dma_start(rel_dram.rearrange("a r c -> r a c"), relT[:, :].rearrange("r (a c) -> r a c", a=F)), 16))
    need(dve, s_load.by(sp.dma_start(relT[:, :], rel_dram.rearrange("a r c -> (a r c)").rearrange("(r k) -> r k", k=256)), 16))
    tok = link(dve, dve.tensor_copy(relO[:, :].rearrange("r (o i) -> r o i", i=F), relT[:, :].rearrange("r (i o) -> r o i", o=F)))
    rel, tok = split_matrix(l3, "rel", R90, relO[:, :], [tok])
    need(pe, tok)
    nc.all_engine_barrier()
    pre.close()
    edge_layer("L3", R90, t["type_90"], rel, m3_dram, attr=t["he"], u=t_u)
    nc.all_engine_barrier()
    M = [sb(l3, f"M{i}", [P, NT, 2 * F]) for i in range(2)]
    for i in range(2):
        m_tok = s_load.by(sp.dma_start(M[i][:, :, :], m3_dram[i, 0:NP, :].rearrange("(t p) f -> p t f", p=P)), 16)
    link(dve, dve.tensor_tensor(q1[:, :, :], H[:, :, :], under(t_u[:, 2 * F:3 * F], NT), ALU.mult))
    link(dve, dve.tensor_reduce(mean[:, :], q1[:, :, :], AX.X, ALU.add))
    need(dve, m_tok)
    link(dve, dve.tensor_tensor(M[0][:, :, :], M[0][:, :, :], M[1][:, :, :], ALU.add))
    link(dve, dve.tensor_tensor(q1[:, :, :], M[0][:, :, 0:F], over(mean[:, :], F), ALU.mult))
    link(dve, dve.tensor_tensor(q1[:, :, :], q1[:, :, :], M[0][:, :, F:2 * F], ALU.add))
    x_tok = link(dve, dve.tensor_tensor(X[:, :, :], X[:, :, :], q1[:, :, :], ALU.add))
    need(sp, x_tok)
    full = (N // P) * P
    stored = s_load.by(sp.dma_start(out[0:full, :].rearrange("(t p) f -> p t f", p=P), X[:, 0:N // P, :]), 16)
    stored = s_load.by(sp.dma_start(out[full:N, :], X[0:N - full, N // P, :]), 16)
    need(sp, stored)
    l3.close()
    life.close()


def layout(inputs):
    import numpy as np

    a = {k: np.asarray(v) for k, v in inputs.items()}
    pad = EP - E
    x = np.zeros((NP, F), np.float32)
    x[:N] = a["x"]
    src = np.concatenate([a["src"].astype(np.int32), np.arange(pad, dtype=np.int32)])
    dst = np.concatenate([a["dst"].astype(np.int32), N + (np.arange(pad, dtype=np.int32) * (NP - N)) // pad])
    tiles = lambda v: np.ascontiguousarray(v.reshape(ET, P).T)
    none = np.full(P, -1, np.int32)
    zeros = np.zeros(pad, np.int32)
    he = np.zeros((EP, F), np.float32)
    he[:E] = a["edge_attr_16"]
    d = {
        "x": x, "src_pm": tiles(src), "dst_pm": tiles(dst), "dst_base": dst[::SE][None],
        "src_row": np.concatenate([none, src, none])[None], "dst_row": np.concatenate([none, dst, none])[None],
        "type_8": np.concatenate([a["edge_type_8"], zeros])[None], "type_90": np.concatenate([a["edge_type_90"], zeros])[None],
        "he": he.reshape(SG, SUP, P, F).transpose(0, 2, 1, 3).reshape(SG, P, SUP * F),
    }
    eye = np.eye(64, dtype=np.float32)
    g = lambda k: a["L0_gnn_" + k]
    ih, hh, bi, bh = (a["L1_gnn_" + k] for k in ("w_ih", "w_hh", "b_ih", "b_hh"))
    gru = np.zeros((2 * F + 2, 4 * F), np.float32)
    gru[0:F, 0:3 * F] = ih.T
    gru[F:2 * F, 0:2 * F] = hh[0:2 * F].T
    gru[F:2 * F, 3 * F:] = hh[2 * F:].T
    gru[2 * F, 0:3 * F] = bi
    gru[2 * F + 1, 0:2 * F] = bh[0:2 * F]
    gru[2 * F + 1, 3 * F:] = bh[2 * F:]
    ws = {
        "enc0": np.concatenate([g("enc_W0")] * 2), "enc1": np.concatenate([g("enc_W1")] * 2), "enc2": g("enc_W2"),
        "dec0": np.concatenate([g("dec_W0")] * 2), "dec1": g("dec_W1"), "dec2": g("dec_W2"),
        "lat0": g("lat_W0"), "lat1": g("lat_W1"), "dfc0": g("dfc_W0"), "dfc1": g("dfc_W1"),
        "eye64": eye, "fold64": np.concatenate([eye] * 2), "fold16": np.concatenate([eye[0:F, 0:F]] * 2),
        "gcn": a["L2_gnn_W"], "gcn_b": a["L2_gnn_b"][:, None], "gru": gru, "emb": a["L1_gnn_edge_emb"],
        "w_comp": a["L3_gnn_w_comp"].T, "V": a["L3_gnn_weight"].reshape(F, 30, F).transpose(1, 0, 2).reshape(30, F * F),
        "ws": a["L3_gnn_Ws"],
    }
    for i in range(3):
        ws[f"wa{i}"] = np.repeat(a["L3_gnn_Wa"][0, i * F:(i + 1) * F][:, None], P, 1)
    for k in ("enc_b0", "enc_b1", "enc_b2", "lat_b0", "lat_b1", "dfc_b0", "dfc_b1", "dec_b0", "dec_b1", "dec_b2"):
        ws[k] = g(k)[:, None]
    cols, at = {}, 0
    pack = np.zeros((P, sum(v.shape[1] for v in ws.values())), np.float32)
    for k, v in ws.items():
        cols[k] = (v.shape[0], at, at + v.shape[1])
        pack[:v.shape[0], at:at + v.shape[1]] = v
        at += v.shape[1]
    d["wpack"] = pack
    return {k: np.ascontiguousarray(v) for k, v in d.items()}, cols


def kernel(**inputs):
    import concourse.bacc as bacc
    from concourse.bass_utils import run_bass_kernel_spmd

    nc = bacc.Bacc("TRN2", target_bir_lowering=False, num_devices=1)
    arrays, cols = layout(inputs)
    t = {k: nc.dram_tensor(f"in_{k}", v.shape, mybir.dt.from_np(v.dtype), kind="ExternalInput").ap() for k, v in arrays.items()}
    out = nc.dram_tensor("out_x", (N, F), F32, kind="ExternalOutput").ap()
    program(nc, t, cols, out)
    r = run_bass_kernel_spmd(nc, [{f"in_{k}": v for k, v in arrays.items()}], core_ids=[0])
    return r.results[0]["out_x"]
```

```python
import concourse.bass as bass
from concourse import mybir
from contextlib import ExitStack

F32, BF16, F16, I32, U32 = mybir.dt.float32, mybir.dt.bfloat16, mybir.dt.float16, mybir.dt.int32, mybir.dt.uint32
FP8, U8 = mybir.dt.float8e4, mybir.dt.uint8
ALU = mybir.AluOpType
ACT = mybir.ActivationFunctionType
AX = mybir.AxisListType

P = 128
N, E, F = 6250, 206250, 16
NT = -(-N // P)
NP = NT * P
SUP = 8
BODY = 2 * SUP
ITS = -(-E // (P * BODY))
ET = ITS * BODY
EP = ET * P
SG = ET // SUP
SE = SUP * P
MROWS = NP + 2 * 64
SHIFT = 13
ROW = 1 << SHIFT
R8, R90 = 8, 90
MANY = 1024
BITS = 16
CH = 448
HALF = 7
RING = 7
TG = 7
EPS = 1e-5
SLOPE = 0.01
WIN = 64
ONE_FP8 = 0x38
ZCOLS = (0, 896, 3584, NP)
ZITS = NT // 7
TOP = 14
TINY = 2.0 ** -100


class Counted:

    def __init__(self, nc, name):
        self.sem = nc.alloc_semaphore(name)
        self.n = 0

    def by(self, ins, k=1):
        ins.then_inc(self.sem, k)
        self.n += k
        return (self.sem, self.n)


class Looped:

    def __init__(self, nc, name, per=1, step=1):
        self.sem, self.per, self.step, self.n0 = nc.alloc_semaphore(name), per, step, 0

    def credit(self, eng, depth):
        eng.sem_inc(self.sem, depth * self.step)
        self.n0 += depth * self.step

    def credit_dma(self, ins):
        ins.then_inc(self.sem, self.step)
        self.n0 += self.step

    def at(self, it, k):
        return it * (self.per * self.step) + (self.n0 + k * self.step)

    def close(self, its):
        self.n0 += its * self.per * self.step
        return (self.sem, self.n0)


def need(eng, *tokens):
    for sem, value in tokens:
        eng.wait_ge(sem, value)


def program(nc, t, wcols, out):
    pe, dve, act, pool, sp = nc.tensor, nc.vector, nc.scalar, nc.gpsimd, nc.sync
    engines = [pe.engine, dve.engine, act.engine, pool.engine, sp.engine]
    life = ExitStack()

    turns = nc.alloc_semaphore("turns")

    def hold(eng, sem, value):
        eng.wait_ge(sem, value)
        eng.sem_inc(turns, 1)

    done = {e: Counted(nc, f"done_{n}") for e, n in ((pe, "pe"), (dve, "dve"), (act, "act"), (pool, "pool"))}
    s_load = Counted(nc, "loaded")

    def step(eng, ins):
        return done[eng].by(ins)

    def link(eng, ins):
        tok = step(eng, ins)
        need(eng, tok)
        return tok

    def sb(stack, name, shape, dt=F32):
        return stack.enter_context(nc.sbuf_tensor(name, list(shape), dt))

    def banks(stack, name, n):
        return [stack.enter_context(nc.psum_tensor(f"{name}{b}", [P, 512], F32)) for b in range(n)]

    adj = nc.dram_tensor("adj", (NP * ROW, 1), U8).ap()
    adj_rows = adj.rearrange("(r c) o -> r (c o)", c=ROW)
    h_dram = nc.dram_tensor("h_rows", (NP, F), F32).ap()
    m1_dram = nc.dram_tensor("m1_rows", (2, MROWS, F), F32).ap()
    m3_dram = nc.dram_tensor("m3_rows", (2, MROWS, 2 * F), F32).ap()
    v_dram = {c: nc.dram_tensor(f"v_rows{c}", (NP, c), F32).ap() for c in (F, 64)}
    s_dram = {c: nc.dram_tensor(f"s_rows{c}", (MROWS, c), F32).ap() for c in (F, 64)}
    dinv_dram = nc.dram_tensor("dinv_row", (NT, P), F32).ap()
    rel_dram = nc.dram_tensor("rel_flat", (F, R90, F), F32).ap()

    X = sb(life, "X", [P, NT, F])
    W = sb(life, "W", [P, t["wpack"].shape[1]])
    I128 = sb(life, "I128", [P, P])
    dloc = sb(life, "dloc", [P, ET])
    baseI = sb(life, "baseI", [P, SG], I32)
    dinvN = sb(life, "dinvN", [P, NT])
    iotaP = sb(life, "iotaP", [P, 1])
    iotaPi = sb(life, "iotaPi", [P, 1], I32)
    iota128 = sb(life, "iota128", [P, P])
    bitno = sb(life, "bitno", [2 * BITS, 1], I32)
    H = sb(life, "H", [P, NT, F])
    q1 = sb(life, "q1", [P, NT, F])
    mean = sb(life, "mean", [P, NT])
    var = sb(life, "var", [P, NT])
    emb = sb(life, "emb", [R8, 3, 256], BF16)
    rel = sb(life, "rel", [R90, 3, 256], BF16)
    t_u = sb(life, "t_u", [P, 3 * F])
    path = sb(life, "path", [P, 1], I32)

    def w(name):
        r, c0, c1 = wcols[name]
        return W[0:r, c0:c1]

    def over(ap, n):
        return ap.rearrange("p (a o) -> p a o", o=1).to_broadcast([ap.shape[0], ap.shape[1], n])

    def under(ap, n):
        return ap.rearrange("p (o a) -> p o a", o=1).to_broadcast([ap.shape[0], n, ap.shape[1]])

    def norm(x_tok):
        need(dve, x_tok)
        link(dve, dve.tensor_reduce(mean[:, :], X[:, :, :], AX.X, ALU.add))
        link(dve, dve.tensor_scalar(mean[:, :], mean[:, :], 1.0 / F, None, ALU.mult))
        link(dve, dve.tensor_tensor(H[:, :, :], X[:, :, :], over(mean[:, :], F), ALU.subtract))
        link(dve, dve.tensor_tensor(q1[:, :, :], H[:, :, :], H[:, :, :], ALU.mult))
        link(dve, dve.tensor_reduce(var[:, :], q1[:, :, :], AX.X, ALU.add))
        need(act, link(dve, dve.tensor_scalar(var[:, :], var[:, :], 1.0 / F, EPS, ALU.mult, ALU.add)))
        need(dve, step(act, act.activation(var[:, :], var[:, :], ACT.Sqrt)))
        link(dve, dve.reciprocal(var[:, :], var[:, :]))
        return link(dve, dve.scalar_tensor_tensor(H[:, :, :], H[:, :, :], 0.0, over(var[:, :], F), ALU.max, ALU.mult))

    setup = ExitStack()
    dstI = sb(setup, "dstI", [P, ET], I32)
    srcI = sb(setup, "srcI", [P, ET], I32)
    nextI = sb(setup, "nextI", [P, ET], I32)
    gap = sb(setup, "gap", [P, ET])
    bad = sb(setup, "bad", [P, 6])
    allones = sb(setup, "allones", [P, P])
    many = sb(setup, "many", [P, 1])
    most = [sb(setup, f"most{h}", [P, SUP]) for h in range(2)]
    flag = setup.enter_context(nc.psum_tensor("flag", [P, 512], F32))
    iotaH = sb(setup, "iotaH", [P, P], I32)
    zdiag = sb(setup, "zdiag", [P, 2 * NP], U8)
    zf = sb(setup, "zf", [P, 2 * MROWS * F // P])
    zb = sb(setup, "zb", [P, P], BF16)
    link(pool, pool.memset(I128[:, :], 0.0))
    ready = step(pool, pool.affine_select(out=I128[:, :], in_=I128[:, :], compare_op=ALU.not_equal, fill=1.0,
                                          base=0, pattern=[[-1, P]], channel_multiplier=1))
    link(dve, dve.memset(zdiag[:, :].bitcast(I32), 0))
    need(dve, ready)
    need(sp, link(dve, dve.tensor_scalar(zdiag[:, NP:NP + P], I128[:, :], float(ONE_FP8), None, ALU.mult)))
    step(dve, dve.memset(zb[:, :], 0.0))
    need(sp, step(dve, dve.memset(zf[:, :], 0.0)))

    def load(dst, src):
        return s_load.by(act.dma_start(dst, src), 16)

    load(dstI[:, :], t["dst_pm"])
    load(srcI[:, :], t["src_pm"])
    load(nextI[:, :], t["dst_next"])
    load(baseI[:, :], t["dst_base"].to_broadcast([P, SG]))
    load(X[:, :, :], t["x"].rearrange("(t p) f -> p t f", p=P))
    loaded = load(W[:, :], t["wpack"])
    step(pool, pool.iota(iotaPi[:, :], pattern=[[0, 1]], base=0, channel_multiplier=1))
    step(pool, pool.iota(iota128[:, :], pattern=[[1, P]], base=0, channel_multiplier=0, allow_small_or_imprecise_dtypes=True))
    step(pool, pool.iota(iotaH[:, :], pattern=[[1, P]], base=0, channel_multiplier=0))
    ready = (done[pool].sem, done[pool].n)
    s_zero = [Counted(nc, f"zeroed{i}") for i in range(3)]

    def zero(stage, k):
        c0, c1 = ZCOLS[stage], ZCOLS[stage + 1]
        return sp.dma_start(adj_rows[bass.ds(k * P, P), c0:c1], zdiag[:, bass.ds(k * -P + (NP + c0), c1 - c0)]).then_inc(s_zero[stage].sem, 16)

    for k in range(NT):
        zero(0, k)
    s_sums = Counted(nc, "sums_zeroed")

    need(dve, loaded, ready)
    step(dve, dve.tensor_copy(iotaP[:, :], iotaPi[:, :]))
    step(dve, dve.tensor_scalar(bitno[:, :], iotaPi[0:2 * BITS, :], BITS - 1, None, ALU.bitwise_and))
    step(dve, dve.tensor_tensor(dloc[:, :].rearrange("p (s e) -> p s e", e=SUP),
                                dstI[:, :].rearrange("p (s e) -> p s e", e=SUP), over(baseI[:, :], SUP), ALU.subtract))
    step(dve, dve.memset(allones[:, :], 1.0))
    for h in range(2):
        step(dve, dve.memset(most[h][:, :], 0.0))
    link(dve, dve.tensor_tensor(gap[:, :], nextI[:, :], dstI[:, :], ALU.subtract))
    link(dve, dve.tensor_reduce(bad[:, 0:1], gap[:, :], AX.X, ALU.min))
    link(dve, dve.tensor_tensor(gap[:, 0:ET - 1], dstI[:, 1:ET], dstI[:, 0:ET - 1], ALU.subtract))
    link(dve, dve.tensor_reduce(bad[:, 1:2], gap[:, 0:ET - 1], AX.X, ALU.min))
    link(dve, dve.tensor_reduce(bad[:, 2:3], dloc[:, :], AX.X, ALU.max))
    for i in (1, 2):
        link(dve, dve.tensor_reduce(bad[:, 2 + i:3 + i], dstI[:, 0:i * ZITS * BODY], AX.X, ALU.max))
    link(dve, dve.tensor_scalar(bad[:, 0:1], bad[:, 0:1], 0.0, None, ALU.is_lt))
    link(dve, dve.tensor_scalar(bad[:, 1:2], bad[:, 1:2], 1.0, None, ALU.is_lt))
    link(dve, dve.tensor_scalar(bad[:, 2:3], bad[:, 2:3], float(WIN), None, ALU.is_ge))
    for i in (1, 2):
        link(dve, dve.tensor_scalar(bad[:, 2 + i:3 + i], bad[:, 2 + i:3 + i], float(ZCOLS[i]), None, ALU.is_ge))
    need(pe, link(dve, dve.tensor_reduce(bad[:, 5:6], bad[:, 0:5], AX.X, ALU.add)))
    need(dve, step(pe, pe.matmul(flag[:, 0:1], allones[:, :], bad[:, 5:6], start=True, stop=True)))
    link(dve, dve.tensor_scalar(many[:, :], flag[:, 0:1], 0.0, float(MANY), ALU.is_equal, ALU.mult))
    h_tok = norm(loaded)

    def split_matrix(T, r, src):
        link(dve, dve.tensor_copy(T[:, 0, :], src))
        link(dve, dve.tensor_tensor(r, src, T[:, 0, :], ALU.subtract))
        link(dve, dve.tensor_copy(T[:, 1, :], r))
        link(dve, dve.tensor_tensor(T[:, 2, :], r, T[:, 1, :], ALU.subtract))

    relT = sb(setup, "relT", [R90, 256])
    relO = sb(setup, "relO", [R90, 256])
    rel_ps = setup.enter_context(nc.psum_tensor("rel_ps", [P, 512], F32))
    need(pe, loaded)
    pe.matmul(rel_ps[0:R90, 0:256], w("w_comp"), w("V"), start=True, stop=True)
    for i in range(3):
        ins = pe.matmul(rel_ps[:, 256 + i * F:256 + (i + 1) * F], w(f"wa{i}"), w("ws"), start=True, stop=True)
    need(dve, step(pe, ins))
    need(act, step(dve, dve.tensor_copy(relT[:, :], rel_ps[0:R90, 0:256])))
    link(dve, dve.tensor_copy(t_u[:, :], rel_ps[:, 256:256 + 3 * F]))
    need(act, s_load.by(act.dma_start(rel_dram.rearrange("a r c -> r a c"), relT[:, :].rearrange("r (a c) -> r a c", a=F)), 16))
    rel_back = s_load.by(act.dma_start(relO[:, :], rel_dram.rearrange("a r c -> (a r c)").rearrange("(r k) -> r k", k=256)), 16)
    need(dve, rel_back)
    split_matrix(emb, relT[0:R8, :], w("emb"))
    link(dve, dve.tensor_copy(relT[:, :].rearrange("r (o i) -> r o i", i=F), relO[:, :].rearrange("r (i o) -> r o i", o=F)))
    split_matrix(rel, relO[:, :], relT[:, :])

    build = ExitStack()
    SPAN = SE + 2 * P
    keyrow = [sb(build, f"keyrow{h}", [2 * BITS, SPAN], I32) for h in range(2)]
    keybit = [sb(build, f"keybit{h}", [2 * BITS, SPAN], I32) for h in range(2)]
    keypm = [sb(build, f"keypm{h}", [2 * BITS, SPAN], BF16) for h in range(2)]
    hit = sb(build, "hit", [P, 4, 3 * P], BF16)
    cnt = [sb(build, f"cnt{h}", [P, SUP]) for h in range(2)]
    same = [sb(build, f"same{h}", [P, SUP]) for h in range(2)]
    val = [sb(build, f"val{h}", [P, SUP], FP8) for h in range(2)]
    cell = [sb(build, f"cell{h}", [P, SUP], U32) for h in range(2)]
    later = [sb(build, f"later{h}", [P, SUP], I32) for h in range(2)]
    away = [sb(build, f"away{h}", [P, SUP], I32) for h in range(2)]
    spare = sb(build, "spare", [P, ET], I32)
    rank = sb(build, "rank", [P, 3 * P])
    dlo = sb(build, "dlo", [P, ET], I32)
    dhi = sb(build, "dhi", [P, ET], I32)
    ohlo = [sb(build, f"ohlo{h}", [P, SUP, P], BF16) for h in range(2)]
    ohhi = [sb(build, f"ohhi{h}", [P, SUP, NT], BF16) for h in range(2)]
    NDOT = 4
    dot = banks(build, "dot", NDOT)
    hist = build.enter_context(nc.psum_tensor("hist", [P, 512], F32))
    assert NP + ET <= ROW and MANY > 3 * P
    step(pool, pool.iota(spare[:, :], pattern=[[1, ET]], base=NP, channel_multiplier=ROW))
    step(pool, pool.memset(rank[:, 0:P], float(MANY)))
    link(pool, pool.memset(rank[:, P:2 * P], float(MANY + 1)))
    step(pool, pool.memset(rank[:, 2 * P:3 * P], 1.0))
    need(dve, step(pool, pool.affine_select(out=rank[:, P:2 * P], in_=rank[:, P:2 * P], compare_op=ALU.is_gt, fill=1.0,
                                            base=0, pattern=[[-1, P]], channel_multiplier=1)))
    step(dve, dve.tensor_scalar(dlo[:, :], dstI[:, :], P - 1, None, ALU.bitwise_and))
    cols = link(dve, dve.tensor_scalar(dhi[:, :], dstI[:, :], 7, None, ALU.logical_shift_right))

    b_row = [Looped(nc, f"b_row{h}", 2, 16) for h in range(2)]
    b_bit = Looped(nc, "b_bit", 2)
    b_pm = Looped(nc, "b_pm", 2)
    b_oh = Looped(nc, "b_oh", 2)
    b_dot = Looped(nc, "b_dot", BODY)
    b_mm = Looped(nc, "b_mm", 2)
    b_cnt = Looped(nc, "b_cnt", BODY)
    b_key = Looped(nc, "b_key", 2 * 8)
    b_val = Looped(nc, "b_val", 2)
    b_sc = [Looped(nc, f"b_sc{h}", SUP, 16) for h in range(2)]
    b_bit.credit(dve, 2)
    b_pm.credit(act, 2)
    b_mm.credit(pe, 2)
    b_cnt.credit(dve, NDOT)
    b_key.credit(dve, 8)
    for h in range(2):
        b_sc[h].credit_dma(pool.dma_start(cell[h][:, :], t["src_pm"][:, 0:SUP].bitcast(U32)))
    need(pe, cols)
    step(pe, pe.matmul(hist[:, 0:NT], zb[:, 0:P], zb[:, 0:NT], start=True, stop=False, skip_group_check=True))
    need(dve, cols)

    def build_edges(it, stage, i0):
        for h in range(2):
            k = 2 * it + h
            sp.wait_ge(b_bit.sem, b_bit.at(it, h - 1))
            win = bass.ds(k * SE, SPAN)
            sp.dma_start(keyrow[h][0:BITS, :], t["src_row"][:, win].to_broadcast([BITS, SPAN])).then_inc(b_row[h].sem, 16)
            sp.dma_start(keyrow[h][BITS:2 * BITS, :], t["dst_row"][:, win].to_broadcast([BITS, SPAN])).then_inc(b_row[h].sem, 16)
            if stage < 2:
                for j in range(4 * h, 4 + 3 * h):
                    zero(stage + 1, it * 7 + (j - i0 * 7))
            dve.wait_ge(b_pm.sem, b_pm.at(it, h - 1))
            dve.wait_ge(b_row[h].sem, b_row[h].at(it, 2))
            dve.tensor_scalar(keybit[h][:, :], keyrow[h][:, :], bitno[:, 0:1], 1,
                              ALU.logical_shift_right, ALU.bitwise_and).then_inc(b_bit.sem, 1)
            act.wait_ge(b_mm.sem, b_mm.at(it, h - 1))
            act.wait_ge(b_bit.sem, b_bit.at(it, h + 1))
            act.activation(keypm[h][:, :], keybit[h][:, :], ACT.Copy, bias=-1.0, scale=2.0).then_inc(b_pm.sem, 1)
            dve.wait_ge(b_mm.sem, b_mm.at(it, h - 1))
            e8 = bass.ds(k * SUP, SUP)
            dve.tensor_tensor(ohlo[h][:, :, :], under(iotaH[:, :], SUP), over(dlo[:, e8], P), ALU.is_equal)
            dve.tensor_tensor(ohhi[h][:, :, :], under(iotaH[:, 0:NT], SUP), over(dhi[:, e8], NT),
                              ALU.is_equal).then_inc(b_oh.sem, 1)
            hold(pe, b_pm.sem, b_pm.at(it, h + 1))
            for j in range(SUP):
                i = h * SUP + j
                hold(pe, b_cnt.sem, b_cnt.at(it, i + 1 - NDOT))
                pe.matmul(dot[j % NDOT][:, 0:3 * P], keypm[h][:, (j + 1) * P:(j + 2) * P], keypm[h][:, j * P:(j + 3) * P],
                          start=True, stop=True).then_inc(b_dot.sem, 1)
            hold(pe, b_oh.sem, b_oh.at(it, h + 1))
            for j in range(SUP):
                ins = pe.matmul(hist[:, 0:NT], ohlo[h][:, j, :], ohhi[h][:, j, :], start=False, stop=False,
                                skip_group_check=True)
            ins.then_inc(b_mm.sem, 1)
            dve.wait_ge(b_key.sem, b_key.at(it, 8 * h))
            for j in range(SUP):
                i = h * SUP + j
                dve.wait_ge(b_dot.sem, b_dot.at(it, i + 1))
                dve.scalar_tensor_tensor(hit[:, j % 4, :], dot[j % NDOT][:, 0:3 * P], float(2 * BITS), rank[:, :],
                                         ALU.is_equal, ALU.mult, accum_out=cnt[h][:, j:j + 1]).then_inc(b_cnt.sem, 1)
            dve.wait_ge(b_sc[h].sem, b_sc[h].at(it, 0))
            dve.tensor_tensor(same[h][:, :], srcI[:, e8], dstI[:, e8], ALU.is_equal).then_inc(b_key.sem, 1)
            dve.tensor_scalar(cell[h][:, :].bitcast(I32), srcI[:, e8], SHIFT, None, ALU.logical_shift_left).then_inc(b_key.sem, 1)
            dve.wait_ge(b_cnt.sem, b_cnt.at(it, (h + 1) * SUP))
            c8 = cell[h][:, :].bitcast(I32)
            hold(dve, b_key.sem, b_key.at(it, 8 * h + 2))
            dve.tensor_tensor(val[h][:, :], cnt[h][:, :], same[h][:, :], ALU.add, saturate=False).then_inc(b_key.sem, 1)
            dve.tensor_tensor(c8, c8, dstI[:, e8], ALU.bitwise_or).then_inc(b_key.sem, 1)
            dve.tensor_scalar(later[h][:, :], cnt[h][:, :], many[:, 0:1], -1.0, ALU.is_ge, ALU.mult).then_inc(b_key.sem, 1)
            dve.tensor_tensor(most[h][:, :], most[h][:, :], cnt[h][:, :], ALU.max).then_inc(b_key.sem, 1)
            dve.wait_ge(b_key.sem, b_key.at(it, 8 * h + 6))
            dve.tensor_tensor(away[h][:, :], later[h][:, :], spare[:, e8], ALU.bitwise_and).then_inc(b_key.sem, 1)
            dve.scalar_tensor_tensor(c8, later[h][:, :], -1, c8, ALU.bitwise_xor, ALU.bitwise_and).then_inc(b_key.sem, 1)
            dve.wait_ge(b_key.sem, b_key.at(it, 8 * h + 8))
            dve.tensor_tensor(c8, c8, away[h][:, :], ALU.bitwise_or).then_inc(b_val.sem, 1)
            hold(pool, b_val.sem, b_val.at(it, h + 1))
            for j in range(SUP):
                pool.indirect_dma_start(adj, bass.IndirectOffsetOnAxis(ap=cell[h][:, j:j + 1], axis=0),
                                        val[h][:, j:j + 1].bitcast(U8), None).then_inc(b_sc[h].sem, 16)

    for stage, (i0, i1) in enumerate(((0, ZITS), (ZITS, 2 * ZITS), (2 * ZITS, ITS))):
        if stage == 2:
            for m in (m1_dram, m3_dram[0:1], m3_dram[1:2]):
                s_sums.by(sp.dma_start(m.rearrange("s n c -> (s n c)").rearrange("(p k) -> p k", p=P), zf[:, :]), 16)
        pool.wait_ge(s_zero[stage].sem, 16 * NT)
        with nc.Fori(i0, i1, engines=engines) as it:
            build_edges(it, stage, i0)
    scattered = [s.close(ITS) for s in b_sc]
    counted = b_mm.close(ITS)
    need(dve, counted)
    link(dve, dve.tensor_scalar(dinvN[:, :], hist[:, 0:NT], 1.0, None, ALU.add))
    need(act, (done[dve].sem, done[dve].n))
    need(dve, step(act, act.activation(dinvN[:, :], dinvN[:, :], ACT.Sqrt)))
    need(pe, link(dve, dve.reciprocal(dinvN[:, :], dinvN[:, :])))
    need(dve, step(pe, pe.transpose(dot[0][0:NT, 0:P], dinvN[:, :], I128[:, :])))
    dinvT = sb(build, "dinvT", [NT, P])
    need(sp, step(dve, dve.tensor_copy(dinvT[:, :], dot[0][0:NT, 0:P])))
    need(sp, s_load.by(sp.dma_start(dinv_dram, dinvT[:, :]), 16))
    need(sp, *scattered)
    need(sp, (s_sums.sem, s_sums.n))
    link(dve, dve.tensor_tensor(most[0][:, :], most[0][:, :], most[1][:, :], ALU.max))
    link(dve, dve.tensor_reduce(bad[:, 0:1], most[0][:, :], AX.X, ALU.max))
    need(pe, link(dve, dve.scalar_tensor_tensor(bad[:, 1:2], bad[:, 0:1], float(15 * MANY), bad[:, 5:6], ALU.is_ge, ALU.add)))
    need(dve, step(pe, pe.matmul(flag[:, 0:1], allones[:, :], bad[:, 1:2], start=True, stop=True)))
    link(dve, dve.tensor_scalar(path[:, :], flag[:, 0:1], 0.0, None, ALU.is_equal))
    nc.all_engine_barrier()
    build.close()
    setup.close()

    def layers(fast, h_tok):
        tag = "" if fast else "g_"
        def dense_scope(name):
            s = ExitStack()
            onerow = sb(s, f"{name}_onerow", [1, P])
            if not fast:
                link(dve, dve.memset(onerow[:, :], 1.0))
                return dict(
                    onerow=onerow,
                    Y=sb(s, f"{name}_Y", [P, NP]),
                    tmp=sb(s, f"{name}_tmp", [P, NT, 64]),
                    ps=banks(s, f"{name}_ps", 6),
                    free={},
                    stack=s)
            d = dict(
                ring=[sb(s, f"{name}_ring{j}", [P, HALF * CH], U8) for j in range(RING)],
                Y=sb(s, f"{name}_Y", [P, NP]),
                T=sb(s, f"{name}_T", [P, NT, 2 * 64], F16),
                peak=sb(s, f"{name}_peak", [P, NT // TG + 1]),
                top=sb(s, f"{name}_top", [1, 4]),
                scale=sb(s, f"{name}_scale", [P, 2]),
                onerow=onerow,
                tmp=sb(s, f"{name}_tmp", [P, NT, 64]),
                dinvB=sb(s, f"{name}_dinvB", [P, NP]),
                ps=banks(s, f"{name}_ps", 8),
                stage=[sb(s, f"{name}_stage{j}", [P, 2 * 64], F16) for j in range(RING)],
                s_stage=Counted(nc, f"{name}_staged"),
                s_in=[Counted(nc, f"{name}_in{j}") for j in range(RING)],
                s_row=Counted(nc, f"{name}_row"),
                free={},
                stack=s)
            s_d = Counted(nc, f"{name}_dinv")
            step(dve, dve.memset(d["onerow"][:, :], 1.0))
            flat = dinv_dram.rearrange("(o t) p -> o (t p)", o=1)
            d["dinv_tok"] = s_d.by(act.dma_start(d["dinvB"][:, :], flat.to_broadcast([P, NP])), 16)
            return d

        def scaled_rows(d, Fo, sources, free, leaky):
            need(dve, *free)
            for g in range(NT // TG):
                src, toks = sources(g)
                need(dve, *toks)
                tok = link(dve, dve.tensor_tensor(d["tmp"][:, g * TG:(g + 1) * TG, 0:Fo], src,
                                                  over(dinvN[:, g * TG:(g + 1) * TG], Fo), ALU.mult))
            if leaky:
                v = d["tmp"][:, :, 0:Fo]
                tok = link(dve, dve.scalar_tensor_tensor(v, v, SLOPE, v, ALU.mult, ALU.max))
            return [tok]

        def edge_sums(name, rows_dram, sums_dram, C, typed=None):
            s = ExitStack()
            R, types, table, attr, u = typed if typed else (1, None, None, None, None)
            Cs = C if attr is None else 2 * C
            srcT = sb(s, f"{name}_src", [P, 1], U32)
            dstT = sb(s, f"{name}_dst", [P, 1], I32)
            dstR = sb(s, f"{name}_dstrow", [P, P], I32)
            dstF = sb(s, f"{name}_dstf", [P, 1])
            rowsG = sb(s, f"{name}_rows", [P, C])
            equal = sb(s, f"{name}_equal", [P, P])
            ahead = sb(s, f"{name}_ahead", [P, P])
            hits = sb(s, f"{name}_hits", [P, P])
            nth = sb(s, f"{name}_nth", [P, 1])
            spare = sb(s, f"{name}_spare", [P, 1])
            to = sb(s, f"{name}_to", [P, 2])
            toU = sb(s, f"{name}_tou", [P, 1], U32)
            total = sb(s, f"{name}_total", [P, Cs])
            pst = banks(s, f"{name}_pst", 2)
            ins_ = 3
            if typed:
                typeR = sb(s, f"{name}_types", [R, P], I32)
                typeH = sb(s, f"{name}_onehot", [R, P], BF16)
                prod = sb(s, f"{name}_prod", [P, F, F])
                msg = sb(s, f"{name}_msg", [P, Cs])
                ins_ += 1
            if attr is not None:
                he = sb(s, f"{name}_he", [P, F])
                part = sb(s, f"{name}_part", [P, 2 * F])
                e_ = sb(s, f"{name}_e", [P, 1])
                ins_ += 1
            link(pool, pool.memset(ahead[:, :], 1.0))
            need(dve, step(pool, pool.affine_select(out=ahead[:, :], in_=ahead[:, :], compare_op=ALU.is_gt, fill=0.0,
                                                    base=0, pattern=[[-1, P]], channel_multiplier=1)))
            step(dve, dve.tensor_scalar(spare[:, :], iotaP[:, :], float(NP), None, ALU.add))
            nv = 6 + (3 if typed else 0) + (4 if attr is not None else 0) + 1
            v_in = Looped(nc, f"{name}_in", ins_, 16)
            v_g = Looped(nc, f"{name}_g", 1, 16)
            v_v = Looped(nc, f"{name}_v", nv)
            v_p = Looped(nc, f"{name}_p", 2 if typed else 1)
            v_s = Looped(nc, f"{name}_s", 1, 16)
            v_s.credit_dma(pool.dma_start(rowsG[:, :], rows_dram[0:P, :]))

            with nc.Fori(0, SG, engines=engines) as sup:
                with nc.Fori(0, SUP, engines=engines) as j:
                    it = sup * SUP + j
                    at = [0]

                    def v(ins):
                        ins.then_inc(v_v.sem, 1)
                        at[0] += 1
                        hold(dve, v_v.sem, v_v.at(it, at[0]))
                        return at[0]

                    hold(sp, v_s.sem, v_s.at(it, 0))
                    with nc.allow_non_contiguous_dma(reason="a column of indices"):
                        sp.dma_start(srcT[:, :], t["src_pm"][:, bass.ds(it, 1)].bitcast(U32)).then_inc(v_in.sem, 16)
                        sp.dma_start(dstT[:, :], t["dst_pm"][:, bass.ds(it, 1)]).then_inc(v_in.sem, 16)
                    sp.dma_start(dstR[:, :], t["dst_row"][:, bass.ds(it * P + P, P)].to_broadcast([P, P])).then_inc(v_in.sem, 16)
                    if typed:
                        sp.dma_start(typeR[:, :], types[:, bass.ds(it * P, P)].to_broadcast([R, P])).then_inc(v_in.sem, 16)
                    if attr is not None:
                        sp.dma_start(he[:, :], attr[bass.ds(sup, 1), :, bass.ds(j * F, F)].rearrange("o p c -> p (o c)")).then_inc(v_in.sem, 16)
                    hold(pool, v_in.sem, v_in.at(it, ins_))
                    pool.indirect_dma_start(rowsG[:, :], None, rows_dram,
                                            bass.IndirectOffsetOnAxis(ap=srcT[:, 0:1], axis=0)).then_inc(v_g.sem, 16)
                    hold(dve, v_in.sem, v_in.at(it, ins_))
                    if typed:
                        onehot = v(dve.tensor_scalar(typeH[:, :], typeR[:, :], iotaP[0:R, :], None, ALU.is_equal))
                    v(dve.tensor_copy(dstF[:, :], dstT[:, :]))
                    v(dve.tensor_scalar(equal[:, :], dstR[:, :], dstF[:, 0:1], None, ALU.is_equal))
                    v(dve.scalar_tensor_tensor(hits[:, :], dstR[:, :], dstF[:, 0:1], ahead[:, :], ALU.is_equal, ALU.mult,
                                               accum_out=nth[:, 0:1]))
                    v(dve.tensor_tensor(to[:, 0:1], dstF[:, :], spare[:, :], ALU.subtract))
                    v(dve.scalar_tensor_tensor(to[:, 1:2], nth[:, :], 0.0, to[:, 0:1], ALU.is_equal, ALU.mult))
                    v(dve.tensor_tensor(toU[:, :].bitcast(I32), to[:, 1:2], spare[:, :], ALU.add))
                    hold(dve, v_g.sem, v_g.at(it, 1))
                    if typed:
                        hold(dve, v_p.sem, v_p.at(it, 1))
                        v(dve.tensor_tensor(prod[:, :, :], pst[1][:, 0:F * F].rearrange("p (o i) -> p o i", i=F), under(rowsG[:, :], F), ALU.mult))
                        last = v(dve.tensor_reduce(msg[:, 0:F], prod[:, :, :], AX.X, ALU.add))
                    if attr is not None:
                        v(dve.tensor_tensor(part[:, 0:F], rowsG[:, :], u[:, 0:F], ALU.mult))
                        v(dve.tensor_tensor(part[:, F:2 * F], he[:, :], u[:, F:2 * F], ALU.mult))
                        v(dve.tensor_reduce(e_[:, :], part[:, :], AX.X, ALU.add))
                        last = v(dve.tensor_scalar(msg[:, F:2 * F], msg[:, 0:F], e_[:, 0:1], None, ALU.mult))
                    if typed:
                        hold(pe, v_v.sem, v_v.at(it, onehot))
                        for p in range(3):
                            ins = pe.matmul(pst[1][:, 0:F * F], typeH[:, :], table[:, p, :], start=(p == 0), stop=(p == 2))
                        ins.then_inc(v_p.sem, 1)
                        hold(pe, v_v.sem, v_v.at(it, last))
                    else:
                        hold(pe, v_v.sem, v_v.at(it, 6))
                        hold(pe, v_g.sem, v_g.at(it, 1))
                    pe.matmul(pst[0][:, 0:Cs], equal[:, :], msg[:, :] if typed else rowsG[:, :], start=True, stop=True).then_inc(v_p.sem, 1)
                    hold(dve, v_p.sem, v_p.at(it, 2 if typed else 1))
                    v(dve.tensor_copy(total[:, :], pst[0][:, 0:Cs]))
                    assert at[0] == nv
                    hold(pool, v_v.sem, v_v.at(it, nv))
                    pool.indirect_dma_start(sums_dram, bass.IndirectOffsetOnAxis(ap=toU[:, 0:1], axis=0), total[:, :], None,
                                            compute_op=ALU.add).then_inc(v_s.sem, 16)
            summed = v_s.close(ET)
            need(sp, summed)
            nc.all_engine_barrier()
            s.close()

        def aggregate_edges(d, Fo, table_toks):
            vals, v, m = d["tmp"][:, :, 0:Fo], v_dram[Fo], s_dram[Fo]
            step(dve, dve.memset(d["Y"][:, :], 0.0))
            need(sp, *table_toks, (done[dve].sem, done[dve].n), *d["free"].values())
            s_load.by(sp.dma_start(v.rearrange("(t p) f -> p t f", p=P), vals), 16)
            s_load.by(sp.dma_start(m[0:NP, :].rearrange("(t p) f -> p t f", p=P), vals), 16)
            need(sp, s_load.by(sp.dma_start(m[NP:MROWS, :], d["Y"][:, 0:Fo]), 16))
            nc.all_engine_barrier()
            edge_sums(f"{tag}gcn{s_load.n}", v, m, Fo)
            need(dve, s_load.by(sp.dma_start(vals, m[0:NP, :].rearrange("(t p) f -> p t f", p=P)), 16))
            tok = link(dve, dve.tensor_tensor(vals, vals, over(dinvN[:, :], Fo), ALU.mult))
            return chunkwise([to_features(d, vals, Fo, [tok])[-1]])

        def split_table(d, Fo, sources, free, leaky=False):
            if not fast:
                return scaled_rows(d, Fo, sources, free, leaky)
            T, tmp, peak, top, scale = d["T"], d["tmp"], d["peak"], d["top"], d["scale"]
            need(dve, *free)
            need(act, *free)
            groups = range(NT // TG)
            G = NT // TG

            def part(g, p):
                return T[:, g * TG:(g + 1) * TG, p * Fo:(p + 1) * Fo]

            def tm(g):
                return tmp[:, g * TG:(g + 1) * TG, 0:Fo]

            for g in groups:
                src, toks = sources(g)
                need(dve, *toks)
                link(dve, dve.tensor_tensor(tm(g), src, over(dinvN[:, g * TG:(g + 1) * TG], Fo), ALU.mult))
                if leaky:
                    link(dve, dve.scalar_tensor_tensor(tm(g), tm(g), SLOPE, tm(g), ALU.mult, ALU.max))
                link(dve, dve.tensor_reduce(peak[:, g:g + 1], tm(g), AX.XY, ALU.max, apply_absolute_value=True))
            need(pe, link(dve, dve.tensor_reduce(peak[:, G:G + 1], peak[:, 0:G], AX.X, ALU.max)))
            need(pe, *bank_free(d, 7))
            need(dve, step(pe, pe.transpose(d["ps"][7][0:1, 0:P], peak[:, G:G + 1], I128[:, :])))
            link(dve, dve.tensor_reduce(top[:, 0:1], d["ps"][7][0:1, 0:P], AX.X, ALU.max))
            link(dve, dve.tensor_scalar(top[:, 0:1], top[:, 0:1], TINY, None, ALU.max))
            link(dve, dve.tensor_scalar(top[:, 1:2].bitcast(I32), top[:, 0:1].bitcast(I32), 0x7F800000, None, ALU.bitwise_and))
            link(dve, dve.tensor_scalar(top[:, 2:3].bitcast(I32), top[:, 1:2].bitcast(I32), -1.0, float((254 + TOP) << 23), ALU.mult, ALU.add))
            need(pe, link(dve, dve.tensor_scalar(top[:, 3:4], top[:, 1:2], 2.0 ** -TOP, None, ALU.mult)))
            need(dve, step(pe, pe.matmul(d["ps"][7][:, 256:258], d["onerow"][:, :], top[:, 2:4], start=True, stop=True)))
            sc = link(dve, dve.tensor_copy(scale[:, :], d["ps"][7][:, 256:258]))
            d["free"][7] = sc
            need(act, sc)
            parts = []
            for g in groups:
                need(dve, step(act, act.activation(part(g, 0), tm(g), ACT.Copy, scale=scale[:, 0:1])))
                parts.append(step(dve, dve.scalar_tensor_tensor(part(g, 1), tm(g), scale[:, 0:1], part(g, 0), ALU.mult, ALU.subtract)))
            return parts

        def aggregate(d, Fo, table_toks):
            rows = 2 * Fo
            if not fast:
                return rows, aggregate_edges(d, Fo, table_toks)
            T, ring, ps, s_in, s_row = d["T"], d["ring"], d["ps"], d["s_in"], d["s_row"]
            out = []
            need(pe, table_toks[0], *d["free"].values())
            need(act, table_toks[-1])
            evac = []
            for half in range(2):
                col = half * HALF * CH

                def load_row(j, row_ap):
                    return sp.dma_start(ring[j][:, :], row_ap)

                def products(table, j, first):
                    for c in range(HALF):
                        if first and evac:
                            need(pe, evac[c])
                        a = ring[j][:, c * CH:(c + 1) * CH].bitcast(FP8)
                        ins = pe.matmul(ps[c][0:rows, 0:CH], table, a, start=first, stop=False, skip_group_check=True)
                    return ins

                for j in range(RING):
                    if s_row.n:
                        need(sp, (s_row.sem, s_row.n - RING + j + 1))
                    s_in[j].by(load_row(j, adj_rows[j * P:(j + 1) * P, col:col + HALF * CH]), 16)
                in0 = [s.n for s in s_in]
                row0 = s_row.n
                for j in range(RING):
                    need(pe, (s_in[j].sem, s_in[j].n))
                    s_row.by(products(T[:, j, 0:rows], j, j == 0))
                stage, s_stage = d["stage"], d["s_stage"]
                with nc.Fori(1, NT // RING, engines=[pe.engine, sp.engine, act.engine]) as it:
                    for j in range(RING):
                        sp.wait_ge(s_row.sem, it * RING + (row0 - RING + j + 1))
                        load_row(j, adj_rows[bass.ds(it * (RING * P) + j * P, P), col:col + HALF * CH]).then_inc(s_in[j].sem, 16)
                    for j in range(RING):
                        act.wait_ge(s_row.sem, it * RING + (row0 - RING + j + 1))
                        act.activation(stage[j][:, 0:rows], T[:, bass.ds(it * RING + j, 1), 0:rows].rearrange("p o c -> p (o c)"),
                                       ACT.Copy).then_inc(s_stage.sem, 1)
                    for j in range(RING):
                        hold(pe, s_in[j].sem, it * 16 + in0[j])
                        hold(pe, s_stage.sem, it * RING + (s_stage.n - RING + j + 1))
                        products(stage[j][:, 0:rows], j, False).then_inc(s_row.sem, 1)
                s_stage.n += RING * (NT // RING - 1)
                for j in range(RING):
                    s_in[j].n += 16 * (NT // RING - 1)
                s_row.n += RING * (NT // RING - 1)
                need(dve, (s_row.sem, s_row.n), d["dinv_tok"])
                evac = []
                for c in range(HALF):
                    cc = slice(col + c * CH, col + (c + 1) * CH)
                    d["free"][c] = (done[dve].sem, done[dve].n + 1)
                    evac.append(step(dve, dve.scalar_tensor_tensor(
                        d["Y"][0:rows, cc], ps[c][0:rows, 0:CH], d["scale"][0:rows, 1:2], d["dinvB"][0:rows, cc], ALU.mult, ALU.mult)))
                out += evac
            return rows, out

        def bank_free(d, b):
            return [d["free"][b]] if b in d["free"] else []

        def feature_chunk(d, c, name, rows, Fo, tok, bias, leaky=True):
            Y, b = d["Y"], c % (len(d["ps"]) // 2)
            cc = slice(c * CH, (c + 1) * CH)
            bank = d["ps"][b]
            need(pe, tok, *bank_free(d, b))
            need(act, step(pe, pe.matmul(bank[0:Fo, 0:CH], w(name), Y[0:rows, cc], start=True, stop=True)))
            tok = step(act, act.activation(Y[0:Fo, cc], bank[0:Fo, 0:CH], ACT.Identity, bias=w(bias)))
            d["free"][b] = tok
            if leaky:
                need(dve, tok)
                tok = step(dve, dve.scalar_tensor_tensor(Y[0:Fo, cc], Y[0:Fo, cc], SLOPE, Y[0:Fo, cc], ALU.mult, ALU.max))
            return tok

        def feature_layer(d, *layer, toks, leaky=True):
            name, rows, Fo, bias = layer
            return [feature_chunk(d, c, name, rows, Fo, toks[c], bias, leaky) for c in range(2 * HALF)]

        def ones_row(d, toks):
            need(pool, *toks)
            return step(pool, pool.memset(d["Y"][32:33, :], 1.0))

        def table_from_Y(d, name, Fi, Fo, toks, layer=None, leaky=False):
            ps = d["ps"]
            ready = [] if layer else list(toks)
            PER = 2

            def sources(g):
                while len(ready) < min(2 * HALF, (g + 2) * PER):
                    c = len(ready)
                    ready.append(feature_chunk(d, c, layer[0], layer[1], layer[2], toks[c], layer[3]))
                b = len(ps) // 2 + g % 3
                bank = ps[b]
                need(pe, *ready[g * PER:(g + 1) * PER], *bank_free(d, b))
                for i in range(TG):
                    n = (g * TG + i) * P
                    tok = pe.matmul(bank[:, i * Fo:(i + 1) * Fo], d["Y"][0:Fi, n:n + P], w(name), start=True, stop=True)
                tok = step(pe, tok)
                d["free"][b] = (done[dve].sem, done[dve].n + 1)
                return bank[:, 0:TG * Fo].rearrange("p (t f) -> p t f", f=Fo), [tok]

            return split_table(d, Fo, sources, list(toks), leaky)

        def to_nodes(d, toks, name, rows, bias):
            ps = d["ps"]
            need(pe, *toks)
            per = 512 // F
            for b in range(0, NT, per):
                m = min(per, NT - b)
                bank = ps[b // per]
                need(pe, *bank_free(d, b // per))
                pe.matmul(bank[:, 0:m * F], d["onerow"][:, :], w(bias)[:, 0:m * F], start=True, stop=False, skip_group_check=True)
                for i in range(m):
                    n = (b + i) * P
                    ins = pe.matmul(bank[:, i * F:(i + 1) * F], d["Y"][0:rows, n:n + P], w(name), start=False, stop=i == m - 1,
                                    skip_group_check=True)
                need(dve, step(pe, ins))
                tok = link(dve, dve.tensor_copy(q1[:, b:b + m, :], bank[:, 0:m * F].rearrange("p (t f) -> p t f", f=F)))
            return tok

        def to_features(d, src, Fi, toks):
            outs = []
            need(pe, *toks)
            for b in range(0, NT, 4):
                m = min(4, NT - b)
                at = (b // 4) % len(d["ps"])
                bank = d["ps"][at]
                need(pe, *bank_free(d, at))
                for i in range(m):
                    ins = pe.transpose(bank[0:Fi, i * P:(i + 1) * P], src[:, b + i, :], I128[:, :])
                need(dve, step(pe, ins))
                outs.append(step(dve, dve.tensor_copy(d["Y"][0:Fi, b * P:(b + m) * P], bank[0:Fi, 0:m * P])))
                d["free"][at] = outs[-1]
            return outs

        def chunkwise(toks):
            return [toks[-1]] * (2 * HALF)

        d = dense_scope(tag + "L0")
        table = split_table(d, F, lambda g: (H[:, g * TG:(g + 1) * TG, :], []), [h_tok])
        if fast:
            ones = ones_row(d, [])
        rows, y = aggregate(d, F, table)
        if not fast:
            ones = ones_row(d, y)
        need(pe, ones)
        table = table_from_Y(d, "enc0", rows + 1, 64, y, leaky=True)
        rows, y = aggregate(d, 64, table)
        table = table_from_Y(d, "enc2", 128, 64, y, layer=("enc1", rows, 128, "enc_b1"))
        rows, y = aggregate(d, 64, table)
        y = feature_layer(d, "fold64", rows, 64, "enc_b2", toks=y)
        y = feature_layer(d, "lat0", 64, 32, "lat_b0", toks=y)
        ones = ones_row(d, y)
        y = feature_layer(d, "lat1", 32, 3, "lat_b1", toks=y, leaky=False)
        y = feature_layer(d, "dfc0", 3, 32, "dfc_b0", toks=y)
        need(pe, ones)
        table = table_from_Y(d, "dfc1", 33, 64, y, leaky=True)
        rows, y = aggregate(d, 64, table)
        table = table_from_Y(d, "dec1", 128, 64, y, layer=("dec0", rows, 128, "dec_b0"))
        rows, y = aggregate(d, 64, table)
        table = table_from_Y(d, "dec2", 64, F, y, layer=("fold64", rows, 64, "dec_b1"))
        rows, y = aggregate(d, F, table)
        to_nodes(d, y, "fold16", rows, "dec_b2_row")
        need(act, link(dve, dve.scalar_tensor_tensor(q1[:, :, :], q1[:, :, :], SLOPE, q1[:, :, :], ALU.mult, ALU.max)))
        need(dve, step(act, act.activation(q1[:, :, :], q1[:, :, :], ACT.Tanh)))
        x_tok = link(dve, dve.tensor_tensor(X[:, :, :], X[:, :, :], q1[:, :, :], ALU.add))
        nc.all_engine_barrier()
        d["stack"].close()

        def edge_layer(name, R, types, table, m_dram, attr=None, u=None):
            name = tag + name
            if not fast:
                return edge_sums(name, h_dram, m_dram[0], F, (R, types, table, attr, u))
            s = ExitStack()
            C = F if attr is None else 2 * F
            PAIRS = SUP // 2
            NM = PAIRS if attr is None else PAIRS + 1
            g = [sb(s, f"{name}_g{h}", [P, SUP, F]) for h in range(2)]
            gidx = [sb(s, f"{name}_gi{h}", [P, SUP], U32) for h in range(2)]
            trow = [sb(s, f"{name}_tr{h}", [R, SE], I32) for h in range(2)]
            oht = [sb(s, f"{name}_ot{h}", [R, SE], BF16) for h in range(2)]
            ohw = [sb(s, f"{name}_ow{h}", [P, SUP, WIN]) for h in range(2)]
            prod = [sb(s, f"{name}_pr{q}", [P, 2, F, F]) for q in range(PAIRS)]
            msg = [sb(s, f"{name}_ms{h}", [P, SUP, C]) for h in range(2)]
            sums = [sb(s, f"{name}_su{h}", [WIN, C]) for h in range(2)]
            psw = banks(s, f"{name}_w", PAIRS)
            psa = banks(s, f"{name}_a", 2)
            if attr is not None:
                he = [sb(s, f"{name}_he{h}", [P, SUP, F]) for h in range(2)]
                ea = [sb(s, f"{name}_ea{h}", [P, SUP, F]) for h in range(2)]
                eb = [sb(s, f"{name}_eb{h}", [P, SUP, F]) for h in range(2)]
                e_ = [sb(s, f"{name}_e{h}", [P, SUP]) for h in range(2)]
            L = lambda n, per=2, st=1: Looped(nc, f"{name}_{n}", per, st)
            nr = 1 if attr is None else 2
            e_idx = [L(f"idx{h}", 1, 16) for h in range(2)]
            e_row = [L(f"row{h}", nr, 16) for h in range(2)]
            e_g = [L(f"g{h}", SUP, 16) for h in range(2)]
            e_out = [L(f"out{h}", 1, 16) for h in range(2)]
            e_ot = L("ot")
            e_ow = L("ow")
            e_e = L("e", 8)
            e_w = L("w", 2 * PAIRS)
            e_pr = L("pr", 2 * PAIRS)
            e_msg = L("msg", 2 * NM)
            e_sum = L("sum")
            e_su = L("su")
            for x, eng, depth in ((e_ot, dve, 2), (e_pr, dve, 2 * PAIRS), (e_w, pe, 2 * PAIRS), (e_sum, pe, 2), (e_su, act, 2), (e_msg, dve, 2 * NM)):
                x.credit(eng, depth)
            for h in range(2):
                e_g[h].credit_dma(pool.dma_start(g[h][:, 0, :], h_dram[0:P, :]))
                e_out[h].credit_dma(act.dma_start(sums[h][:, 0:F], h_dram[0:WIN, :]))

            def matrices(it, h):
                hold(pe, e_ot.sem, e_ot.at(it, h + 1))
                for q in range(PAIRS):
                    hold(pe, e_pr.sem, e_pr.at(it, h * PAIRS + q + 1 - PAIRS))
                    for j in (2 * q, 2 * q + 1):
                        for p in range(3):
                            ins = pe.matmul(psw[q][:, (j % 2) * 256:(j % 2 + 1) * 256], oht[h][:, j * P:(j + 1) * P],
                                            table[:, p, :], start=(p == 0), stop=(p == 2))
                    ins.then_inc(e_w.sem, 1)

            def type_onehots(it, h):
                dve.wait_ge(e_row[h].sem, e_row[h].at(it, nr))
                dve.wait_ge(e_w.sem, e_w.at(it, (h - 1) * PAIRS))
                dve.tensor_scalar(oht[h][:, :], trow[h][:, :], iotaP[0:R, :], None, ALU.is_equal).then_inc(e_ot.sem, 1)

            def message_sums(it, h):
                hold(pe, e_ow.sem, e_ow.at(it, h + 1))
                hold(pe, e_su.sem, e_su.at(it, h - 1))
                hold(pe, e_msg.sem, e_msg.at(it, (h + 1) * NM))
                for j in range(SUP):
                    ins = pe.matmul(psa[h][0:WIN, 0:C], ohw[h][:, j, :], msg[h][:, j, :], start=(j == 0), stop=(j == SUP - 1))
                ins.then_inc(e_sum.sem, 1)

            def edges(it, more):
                for h in range(2):
                    k = 2 * it + h
                    sp.wait_ge(e_g[h].sem, e_g[h].at(it, 0))
                    sp.dma_start(gidx[h][:, :], t["src_pm"][:, bass.ds(k * SUP, SUP)].bitcast(U32)).then_inc(e_idx[h].sem, 16)
                    sp.wait_ge(e_ot.sem, e_ot.at(it, h - 1))
                    sp.dma_start(trow[h][:, :], types[:, bass.ds(k * SE, SE)].to_broadcast([R, SE])).then_inc(e_row[h].sem, 16)
                    if attr is not None:
                        sp.wait_ge(e_pr.sem, e_pr.at(it, (h - 1) * PAIRS - PAIRS + 1))
                        sp.dma_start(he[h][:, :, :].rearrange("p e f -> p (e f)"),
                                     attr[bass.ds(k, 1), :, :].rearrange("o p c -> p (o c)")).then_inc(e_row[h].sem, 16)
                    hold(pool, e_idx[h].sem, e_idx[h].at(it, 1))
                    for q in range(PAIRS):
                        hold(pool, e_pr.sem, e_pr.at(it, (h - 2) * PAIRS + q + 1))
                        for j in (2 * q, 2 * q + 1):
                            pool.indirect_dma_start(g[h][:, j, :], None, h_dram,
                                                    bass.IndirectOffsetOnAxis(ap=gidx[h][:, j:j + 1], axis=0)).then_inc(e_g[h].sem, 16)
                    dve.wait_ge(e_sum.sem, e_sum.at(it, h - 1))
                    dve.tensor_tensor(ohw[h][:, :, :], under(iota128[:, 0:WIN], SUP), over(dloc[:, bass.ds(k * SUP, SUP)], WIN),
                                      ALU.is_equal).then_inc(e_ow.sem, 1)
                    dve.wait_ge(e_g[h].sem, e_g[h].at(it, SUP))
                    if attr is not None:
                        dve.tensor_tensor(ea[h][:, :, :], g[h][:, :, :], under(u[:, 0:F], SUP), ALU.mult).then_inc(e_e.sem, 1)
                        dve.tensor_tensor(eb[h][:, :, :], he[h][:, :, :], under(u[:, F:2 * F], SUP), ALU.mult).then_inc(e_e.sem, 1)

                    def product(q):
                        dve.wait_ge(e_w.sem, e_w.at(it, h * PAIRS + q + 1))
                        dve.wait_ge(e_msg.sem, e_msg.at(it, (h - 1) * NM + q + 1))
                        wq = psw[q][:, :].rearrange("p (t o i) -> p t o i", t=2, o=F)
                        gq = g[h][:, 2 * q:2 * q + 2, :].rearrange("p t (z i) -> p t z i", z=1).to_broadcast([P, 2, F, F])
                        dve.tensor_tensor(prod[q][:, :, :, :], wq, gq, ALU.mult).then_inc(e_pr.sem, 1)

                    def message(q):
                        dve.wait_ge(e_pr.sem, e_pr.at(it, h * PAIRS + q + 1))
                        dve.tensor_reduce(msg[h][:, 2 * q:2 * q + 2, 0:F], prod[q][:, :, :, :], AX.X, ALU.add).then_inc(e_msg.sem, 1)

                    product(0)
                    if attr is not None:
                        dve.wait_ge(e_e.sem, e_e.at(it, 4 * h + 2))
                        dve.tensor_tensor(ea[h][:, :, :], ea[h][:, :, :], eb[h][:, :, :], ALU.add).then_inc(e_e.sem, 1)
                    product(1)
                    message(0)
                    product(2)
                    if attr is not None:
                        dve.wait_ge(e_e.sem, e_e.at(it, 4 * h + 3))
                        dve.tensor_reduce(e_[h][:, :], ea[h][:, :, :], AX.X, ALU.add).then_inc(e_e.sem, 1)
                    product(3)
                    if h == 0:
                        type_onehots(it, 1)
                    elif more:
                        type_onehots(it + 1, 0)
                    for q in range(1, PAIRS):
                        message(q)
                    if attr is not None:
                        dve.wait_ge(e_e.sem, e_e.at(it, 4 * h + 4))
                        dve.wait_ge(e_msg.sem, e_msg.at(it, h * NM + PAIRS))
                        dve.tensor_tensor(msg[h][:, :, F:C], msg[h][:, :, 0:F], over(e_[h][:, :], F), ALU.mult).then_inc(e_msg.sem, 1)
                    if h == 0:
                        matrices(it, 1)
                    elif more:
                        matrices(it + 1, 0)
                    message_sums(it, h)
                    base = act.value_load(baseI[0:1, bass.ds(k, 1)], min_val=0, max_val=MROWS - WIN)
                    act.wait_ge(e_out[h].sem, e_out[h].at(it, 0))
                    act.wait_ge(e_sum.sem, e_sum.at(it, h + 1))
                    act.activation(sums[h][:, :], psa[h][0:WIN, 0:C], ACT.Copy).then_inc(e_su.sem, 1)
                    act.wait_ge(e_su.sem, e_su.at(it, h + 1))
                    act.dma_start(m_dram[h, bass.ds(base, WIN), :], sums[h][:, :]).then_inc(e_out[h].sem, 16)

            type_onehots(0, 0)
            matrices(0, 0)
            with nc.Fori(0, ITS - 1, engines=engines) as it:
                edges(it, True)
            edges(ITS - 1, False)
            landed = [x.close(ITS) for x in e_out]
            need(sp, *landed)
            s.close()

        def store_h(tok):
            need(sp, tok)
            tok = s_load.by(sp.dma_start(h_dram.rearrange("(t p) f -> p t f", p=P), H[:, :, :]), 16)
            need(sp, tok)
            need(pool, tok)
            need(act, tok)

        h_tok = norm(x_tok)
        store_h(h_tok)
        l1 = ExitStack()
        edge_layer("L1", R8, t["type_8"], emb, m1_dram)
        nc.all_engine_barrier()
        l1.close()
        gru = ExitStack()
        Z = sb(gru, tag + "gru_in", [P, NT, 2 * F + 2])
        gates = sb(gru, tag + "gates", [P, NT, 4 * F])
        d = dict(Y=sb(gru, tag + "gru_Y", [2 * F + 2, NP]), ps=banks(gru, tag + "gru_ps", 8), free={})
        m = [sb(gru, f"{tag}gru_m{i}", [P, NT, F]) for i in range(2)]
        for i in range(2):
            m_tok = s_load.by(sp.dma_start(m[i][:, :, :], m1_dram[i, 0:NP, :].rearrange("(t p) f -> p t f", p=P)), 16)
        step(dve, dve.memset(Z[:, :, 2 * F:2 * F + 2], 1.0))
        step(dve, dve.tensor_copy(Z[:, :, F:2 * F], H[:, :, :]))
        need(dve, m_tok)
        z_tok = link(dve, dve.tensor_tensor(Z[:, :, 0:F], m[0][:, :, :], m[1][:, :, :], ALU.add))
        y = to_features(d, Z, 2 * F + 2, [z_tok])
        need(pe, y[-1], *d["free"].values())
        for gr in range(NT // TG):
            bank = d["ps"][gr]
            for i in range(TG):
                n = (gr * TG + i) * P
                ins = pe.matmul(bank[:, i * 64:(i + 1) * 64], d["Y"][0:2 * F + 2, n:n + P], w("gru"), start=True, stop=True)
            need(act, step(pe, ins))
            src = bank[:, 0:TG * 64].rearrange("p (t f) -> p t f", f=64)
            g_tok = step(act, act.activation(gates[:, gr * TG:(gr + 1) * TG, :], src, ACT.Copy))
        need(act, g_tok)
        need(dve, step(act, act.activation(gates[:, :, 0:2 * F], gates[:, :, 0:2 * F], ACT.Sigmoid)))
        r_, z_, in_, hn_ = (gates[:, :, i * F:(i + 1) * F] for i in range(4))
        link(dve, dve.tensor_tensor(hn_, hn_, r_, ALU.mult))
        need(act, link(dve, dve.tensor_tensor(in_, in_, hn_, ALU.add)))
        need(dve, step(act, act.activation(in_, in_, ACT.Tanh)))
        link(dve, dve.tensor_tensor(hn_, H[:, :, :], in_, ALU.subtract))
        link(dve, dve.tensor_tensor(hn_, hn_, z_, ALU.mult))
        link(dve, dve.tensor_tensor(hn_, hn_, in_, ALU.add))
        x_tok = link(dve, dve.tensor_tensor(X[:, :, :], X[:, :, :], hn_, ALU.add))
        nc.all_engine_barrier()
        gru.close()

        h_tok = norm(x_tok)
        d = dense_scope(tag + "L2")
        rows, y = aggregate(d, F, split_table(d, F, lambda g: (H[:, g * TG:(g + 1) * TG, :], []), [h_tok]))
        to_nodes(d, y, "gcn", rows, "gcn_b_row")
        x_tok = link(dve, dve.tensor_tensor(X[:, :, :], X[:, :, :], q1[:, :, :], ALU.add))
        nc.all_engine_barrier()
        d["stack"].close()

        h_tok = norm(x_tok)
        store_h(h_tok)
        l3 = ExitStack()
        edge_layer("L3", R90, t["type_90"], rel, m3_dram, attr=t["he"], u=t_u)
        nc.all_engine_barrier()
        M = [sb(l3, f"{tag}M{i}", [P, NT, 2 * F]) for i in range(2)]
        for i in range(2):
            m_tok = s_load.by(sp.dma_start(M[i][:, :, :], m3_dram[i, 0:NP, :].rearrange("(t p) f -> p t f", p=P)), 16)
        link(dve, dve.tensor_tensor(q1[:, :, :], H[:, :, :], under(t_u[:, 2 * F:3 * F], NT), ALU.mult))
        link(dve, dve.tensor_reduce(mean[:, :], q1[:, :, :], AX.X, ALU.add))
        need(dve, m_tok)
        link(dve, dve.tensor_tensor(M[0][:, :, :], M[0][:, :, :], M[1][:, :, :], ALU.add))
        link(dve, dve.tensor_tensor(q1[:, :, :], M[0][:, :, 0:F], over(mean[:, :], F), ALU.mult))
        link(dve, dve.tensor_tensor(q1[:, :, :], q1[:, :, :], M[0][:, :, F:2 * F], ALU.add))
        x_tok = link(dve, dve.tensor_tensor(X[:, :, :], X[:, :, :], q1[:, :, :], ALU.add))
        need(sp, x_tok)
        full = (N // P) * P
        stored = s_load.by(sp.dma_start(out[0:full, :].rearrange("(t p) f -> p t f", p=P), X[:, 0:N // P, :]), 16)
        stored = s_load.by(sp.dma_start(out[full:N, :], X[0:N - full, N // P, :]), 16)
        need(sp, stored)
        l3.close()

    before = [(c, c.n) for c in (*done.values(), s_load)]
    fits = nc.values_load(path[0:1, 0:1], min_val=0, max_val=1)
    with nc.If(fits != 0):
        layers(True, h_tok)
    for c, n in before:
        c.n = n
    with nc.Else():
        layers(False, h_tok)
    life.close()


def layout(inputs):
    import numpy as np

    a = {k: np.asarray(v) for k, v in inputs.items()}
    pad = EP - E
    x = np.zeros((NP, F), np.float32)
    x[:N] = a["x"]
    src = np.concatenate([a["src"].astype(np.int32), np.arange(pad, dtype=np.int32)])
    dst = np.concatenate([a["dst"].astype(np.int32), N + (np.arange(pad, dtype=np.int32) * (NP - N)) // pad])
    tiles = lambda v: np.ascontiguousarray(v.reshape(ET, P).T)
    none = np.full(P, -1, np.int32)
    zeros = np.zeros(pad, np.int32)
    he = np.zeros((EP, F), np.float32)
    he[:E] = a["edge_attr_16"]
    d = {
        "x": x, "src_pm": tiles(src), "dst_pm": tiles(dst), "dst_base": dst[::SE][None],
        "dst_next": tiles(np.concatenate([dst[1:], dst[-1:]])),
        "src_row": np.concatenate([none, src, none])[None], "dst_row": np.concatenate([none, dst, none])[None],
        "type_8": np.concatenate([a["edge_type_8"], zeros])[None], "type_90": np.concatenate([a["edge_type_90"], zeros])[None],
        "he": he.reshape(SG, SUP, P, F).transpose(0, 2, 1, 3).reshape(SG, P, SUP * F),
    }
    eye = np.eye(64, dtype=np.float32)
    g = lambda k: a["L0_gnn_" + k]
    ih, hh, bi, bh = (a["L1_gnn_" + k] for k in ("w_ih", "w_hh", "b_ih", "b_hh"))
    gru = np.zeros((2 * F + 2, 4 * F), np.float32)
    gru[0:F, 0:3 * F] = ih.T
    gru[F:2 * F, 0:2 * F] = hh[0:2 * F].T
    gru[F:2 * F, 3 * F:] = hh[2 * F:].T
    gru[2 * F, 0:3 * F] = bi
    gru[2 * F + 1, 0:2 * F] = bh[0:2 * F]
    gru[2 * F + 1, 3 * F:] = bh[2 * F:]
    ws = {
        "enc0": np.concatenate([g("enc_W0")] * 2 + [g("enc_b0")[None]]), "enc1": np.concatenate([g("enc_W1")] * 2), "enc2": g("enc_W2"),
        "dec0": np.concatenate([g("dec_W0")] * 2), "dec1": g("dec_W1"), "dec2": g("dec_W2"),
        "lat0": g("lat_W0"), "lat1": g("lat_W1"), "dfc0": g("dfc_W0"), "dfc1": np.concatenate([g("dfc_W1"), g("dfc_b1")[None]]),
        "fold64": np.concatenate([eye] * 2), "fold16": np.concatenate([eye[0:F, 0:F]] * 2),
        "gcn": np.concatenate([a["L2_gnn_W"]] * 2), "gcn_b_row": np.tile(a["L2_gnn_b"], 512 // F)[None], "dec_b2_row": np.tile(g("dec_b2"), 512 // F)[None], "gru": gru, "emb": a["L1_gnn_edge_emb"],
        "w_comp": a["L3_gnn_w_comp"].T, "V": a["L3_gnn_weight"].reshape(F, 30, F).transpose(1, 0, 2).reshape(30, F * F),
        "ws": a["L3_gnn_Ws"],
    }
    for i in range(3):
        ws[f"wa{i}"] = np.repeat(a["L3_gnn_Wa"][0, i * F:(i + 1) * F][:, None], P, 1)
    for k in ("enc_b1", "enc_b2", "lat_b0", "lat_b1", "dfc_b0", "dec_b0", "dec_b1"):
        ws[k] = g(k)[:, None]
    cols, at = {}, 0
    pack = np.zeros((P, sum(v.shape[1] for v in ws.values())), np.float32)
    for k, v in ws.items():
        cols[k] = (v.shape[0], at, at + v.shape[1])
        pack[:v.shape[0], at:at + v.shape[1]] = v
        at += v.shape[1]
    d["wpack"] = pack
    return {k: np.ascontiguousarray(v) for k, v in d.items()}, cols


def kernel(**inputs):
    import concourse.bacc as bacc
    from concourse.bass_utils import run_bass_kernel_spmd

    nc = bacc.Bacc("TRN2", target_bir_lowering=False, num_devices=1)
    arrays, cols = layout(inputs)
    t = {k: nc.dram_tensor(f"in_{k}", v.shape, mybir.dt.from_np(v.dtype), kind="ExternalInput").ap() for k, v in arrays.items()}
    out = nc.dram_tensor("out_x", (N, F), F32, kind="ExternalOutput").ap()
    program(nc, t, cols, out)
    r = run_bass_kernel_spmd(nc, [{f"in_{k}": v for k, v in arrays.items()}], core_ids=[0])
    return r.results[0]["out_x"]
```
